# Optimizing a Trainium2 kernel written in Bass

```python
import numpy as np
import jax
import jax.numpy as jnp

def _softmax(x, axis=-1):
    return jax.nn.softmax(x, axis=axis)

def _gelu(x):
    return jax.nn.gelu(x, approximate=True)

def _silu(x):
    return jax.nn.silu(x)

def _sigmoid(x):
    return jax.nn.sigmoid(x)

def _layernorm(x, axis=-1, eps=1e-05):
    m = jnp.mean(x, axis=axis, keepdims=True)
    v = jnp.var(x, axis=axis, keepdims=True)
    return (x - m) / jnp.sqrt(v + eps)

def _scatter_add(tgt, idx, src, axis=0):
    return tgt.at[idx].add(src)

def _segment_sum(src, seg, n):
    return jax.ops.segment_sum(src, seg, n)
kernel_name = 'mk_sandwich_d1_jaxref_r8_8b0dea'

def setup_inputs(seed: int=0):
    np.random.seed(seed)
    _w = jnp.asarray

    def _L0_attn_setup():
        import jax, jax.numpy as jnp
        import numpy as np
        B, N, D = (4, 256, 128)
        THRESHOLD_FACTOR = 1.25

        def _linear(x, W, b):
            return x @ W.T + b
        key = jax.random.key(seed)
        ks = jax.random.split(key, 8)
        s = 0.02
        return {'hidden_states': jax.random.normal(ks[0], (B, N, D), jnp.float32), 'Wq': jax.random.normal(ks[1], (D, D), jnp.float32) * s, 'bq': jnp.zeros((D,), jnp.float32), 'Wk': jax.random.normal(ks[2], (D, D), jnp.float32) * s, 'bk': jnp.zeros((D,), jnp.float32), 'Wv': jax.random.normal(ks[3], (D, D), jnp.float32) * s, 'bv': jnp.zeros((D,), jnp.float32), 'Wo': jax.random.normal(ks[4], (D, D), jnp.float32) * s, 'bo': jnp.zeros((D,), jnp.float32), 'Wtq': jax.random.normal(ks[5], (2, D), jnp.float32) * s, 'btq': jnp.zeros((2,), jnp.float32), 'Wfq': jax.random.normal(ks[6], (D, 2), jnp.float32) * s, 'bfq': jnp.zeros((D,), jnp.float32)}
    _L0_attn_in = _L0_attn_setup()

    def _L0_ffn_setup():
        import jax, jax.numpy as jnp
        import numpy as np
        H = 128
        F = 4 * H
        E = 16
        K = 4
        key = jax.random.key(seed)
        ks = jax.random.split(key, 10)
        s = 0.02
        return {'x': jax.random.normal(ks[0], (2, 128, H), dtype=jnp.float32), 'Wr1': jax.random.normal(ks[1], (H, H), dtype=jnp.float32) * s, 'br1': jnp.zeros((H,), dtype=jnp.float32), 'Wr2': jax.random.normal(ks[2], (H, E), dtype=jnp.float32) * s, 'br2': jnp.zeros((E,), dtype=jnp.float32), 'W1': jax.random.normal(ks[3], (E, H, F), dtype=jnp.float32) * s, 'b1': jnp.zeros((E, F), dtype=jnp.float32), 'W2': jax.random.normal(ks[4], (E, F, H), dtype=jnp.float32) * s, 'b2': jnp.zeros((E, H), dtype=jnp.float32)}
    _L0_ffn_in = _L0_ffn_setup()
    _d = {'L0_attn_hidden_states': _L0_attn_in['hidden_states'], 'L0_attn_Wq': _L0_attn_in['Wq'], 'L0_attn_bq': _L0_attn_in['bq'], 'L0_attn_Wk': _L0_attn_in['Wk'], 'L0_attn_bk': _L0_attn_in['bk'], 'L0_attn_Wv': _L0_attn_in['Wv'], 'L0_attn_bv': _L0_attn_in['bv'], 'L0_attn_Wo': _L0_attn_in['Wo'], 'L0_attn_bo': _L0_attn_in['bo'], 'L0_attn_Wtq': _L0_attn_in['Wtq'], 'L0_attn_btq': _L0_attn_in['btq'], 'L0_attn_Wfq': _L0_attn_in['Wfq'], 'L0_attn_bfq': _L0_attn_in['bfq'], 'L0_ffn_Wr1': _L0_ffn_in['Wr1'], 'L0_ffn_br1': _L0_ffn_in['br1'], 'L0_ffn_Wr2': _L0_ffn_in['Wr2'], 'L0_ffn_br2': _L0_ffn_in['br2'], 'L0_ffn_W1': _L0_ffn_in['W1'], 'L0_ffn_b1': _L0_ffn_in['b1'], 'L0_ffn_W2': _L0_ffn_in['W2'], 'L0_ffn_b2': _L0_ffn_in['b2']}
    _x0 = _d['L0_attn_hidden_states']
    _d['L0_attn_hidden_states'] = jax.random.normal(jax.random.fold_in(jax.random.key(seed), 1), (8, 512, 128), dtype=_x0.dtype)
    del _x0
    return _d

def reference(L0_attn_hidden_states, L0_attn_Wq, L0_attn_bq, L0_attn_Wk, L0_attn_bk, L0_attn_Wv, L0_attn_bv, L0_attn_Wo, L0_attn_bo, L0_attn_Wtq, L0_attn_btq, L0_attn_Wfq, L0_attn_bfq, L0_ffn_Wr1, L0_ffn_br1, L0_ffn_Wr2, L0_ffn_br2, L0_ffn_W1, L0_ffn_b1, L0_ffn_W2, L0_ffn_b2):

    def _L0_attn_ref(hidden_states, Wq, bq, Wk, bk, Wv, bv, Wo, bo, Wtq, btq, Wfq, bfq):
        import jax, jax.numpy as jnp
        import numpy as np
        B, N, D = (4, 256, 128)
        THRESHOLD_FACTOR = 1.25

        def _linear(x, W, b):
            return x @ W.T + b
        d = hidden_states.shape[-1]
        q = _linear(hidden_states, Wq, bq)
        k = _linear(hidden_states, Wk, bk)
        v = _linear(hidden_states, Wv, bv)
        scores = jnp.einsum('bid,bjd->bij', q, k) / jnp.sqrt(jnp.asarray(d, (scores_dtype := q.dtype)))
        qp = _linear(hidden_states, Wtq, btq)
        diff = qp[:, :, None, :] - qp[:, None, :, :]
        dist_sq = jnp.sum(diff * diff, axis=-1)
        phase_diff = jnp.arctan2(diff[..., 1], diff[..., 0])
        forward_bias = 0.5 * (1.0 + jnp.cos(phase_diff))
        mean_dist = jnp.mean(dist_sq, axis=(-1, -2), keepdims=True)
        std_dist = jnp.std(dist_sq, axis=(-1, -2), keepdims=True, ddof=1)
        threshold = mean_dist + THRESHOLD_FACTOR * std_dist
        n = dist_sq.shape[-1]
        causal = jnp.tril(jnp.ones((n, n), bool))
        valid = (dist_sq <= threshold) & causal[None]
        binary_attn = valid.astype(scores.dtype) * forward_bias
        masked = jnp.where(binary_attn == 0, -jnp.inf, scores)
        weights = jax.nn.softmax(masked, axis=-1)
        context = jnp.einsum('bij,bjd->bid', weights, v)
        output = _linear(context, Wo, bo)
        r_embed = qp / jnp.maximum(jnp.linalg.norm(qp, axis=-1, keepdims=True), 1e-12)
        quantum_output = _linear(r_embed, Wfq, bfq)
        return hidden_states + output + 0.1 * quantum_output

    def _L0_ffn_ref(x, Wr1, br1, Wr2, br2, W1, b1, W2, b2):
        import jax, jax.numpy as jnp
        import numpy as np
        H = 128
        F = 4 * H
        E = 16
        K = 4
        B, S, Hd = x.shape
        xf = x.reshape(-1, Hd)
        T = xf.shape[0]
        logits = jnp.maximum(xf @ Wr1 + br1, 0.0) @ Wr2 + br2
        topw, topi = jax.lax.top_k(logits, K)
        topw = jax.nn.softmax(topw, axis=-1)
        c = jnp.zeros((T, E), dtype=xf.dtype)
        c = c.at[jnp.arange(T)[:, None], topi].add(topw)
        h = jax.nn.gelu(jnp.einsum('th,ehf->etf', xf, W1) + b1[:, None, :], approximate=False)
        y = jnp.einsum('etf,efh->eth', h, W2) + b2[:, None, :]
        out = jnp.einsum('eth,te->th', y, c)
        return out.reshape(B, S, Hd)
    x = L0_attn_hidden_states
    x = x + _layernorm(_L0_attn_ref(_layernorm(x, axis=-1), L0_attn_Wq, L0_attn_bq, L0_attn_Wk, L0_attn_bk, L0_attn_Wv, L0_attn_bv, L0_attn_Wo, L0_attn_bo, L0_attn_Wtq, L0_attn_btq, L0_attn_Wfq, L0_attn_bfq), axis=-1)
    x = x + _layernorm(_L0_ffn_ref(_layernorm(x, axis=-1), L0_ffn_Wr1, L0_ffn_br1, L0_ffn_Wr2, L0_ffn_br2, L0_ffn_W1, L0_ffn_b1, L0_ffn_W2, L0_ffn_b2), axis=-1)
    return x

_drawn_inputs = setup_inputs


def setup_inputs(seed=0):
    import zlib

    import numpy as np

    out = dict(_drawn_inputs(seed))
    spreads = {'L0_attn_bq': (0.0, 0.8),
     'L0_attn_bk': (0.0, 0.8),
     'L0_attn_bv': (0.0, 0.274),
     'L0_attn_bo': (0.0, 0.1),
     'L0_attn_btq': (0.0, 0.8),
     'L0_attn_bfq': (0.0, 0.598),
     'L0_ffn_br1': (0.0, 0.1),
     'L0_ffn_br2': (0.0, 0.1),
     'L0_ffn_b1': (0.0, 0.1),
     'L0_ffn_b2': (0.0, 0.1)}
    factors = {'L0_attn_Wq': 8.0,
     'L0_attn_Wk': 8.0,
     'L0_attn_Wv': 6.331,
     'L0_attn_Wtq': 5.646,
     'L0_attn_Wfq': 8.0}
    for name, (base, spread) in spreads.items():
        noise = np.random.default_rng([zlib.crc32(name.encode()), seed]).standard_normal(out[name].shape)
        drawn = base * np.exp(spread * noise) if base else spread * noise
        out[name] = jnp.asarray(drawn.astype(out[name].dtype))
    for name, factor in factors.items():
        out[name] = (out[name] * factor).astype(out[name].dtype)
    return out
```

```python
from contextlib import ExitStack

import concourse.bass as bass
from concourse import mybir

F32 = mybir.dt.float32
F32R = mybir.dt.float32r
BF16 = mybir.dt.bfloat16
U32 = mybir.dt.uint32
ALU = mybir.AluOpType
ACT = mybir.ActivationFunctionType
AX_X = mybir.AxisListType.X

P = 128
EPS = 1e-5
TINY_NORM = 1e-12
THRESHOLD_FACTOR = 1.25
QUANTUM = 0.1
PI_CONE = 2.0 ** -12
MASKED = -(2.0 ** 40)
TOP = 4
EP = 32


def attention_moe_kernel(nc, x_d, Wq, bq, Wk, bk, Wv, bv, Wo, bo, Wtq, btq, Wfq, bfq,
                         Wr1, br1, Wr2, br2, W1, b1, W2, b2, out_d):
    B, N, D = x_d.shape
    E, _, FF = W1.shape
    NT = N // P
    FC = FF // P
    assert D == P and N == 512 and FC == 4 and E == 16 and B == 8
    SCALE = float(D) ** -0.5
    PAIRS = float(N) * float(N)

    cT_d = nc.dram_tensor("cT_scratch", (E, B * N), F32, kind="Internal").ap()

    ctx = ExitStack()
    with ctx:
        def sb(name, shape, dt=F32):
            return ctx.enter_context(nc.sbuf_tensor(name, shape, dt))

        def sem(name):
            return ctx.enter_context(nc.semaphore(name))

        x_sb = sb("x_sb", [P, B * N])
        x_hi = sb("x_hi", [P, B * N], F32R)
        x_lo = sb("x_lo", [P, B * N], F32R)
        acc = sb("acc", [P, B * N])
        ident = sb("ident", [P, P])
        ones = sb("ones", [P, P])
        avg = sb("avg", [P, P])
        mask_w = sb("mask_w", [P, P], BF16)
        tri = sb("tri", [P, P], BF16)
        pick_x = sb("pick_x", [2, P])
        pick_y = sb("pick_y", [2, P])
        iota_e = sb("iota_e", [P, E])
        half = sb("half", [P, NT])
        mhalf = sb("mhalf", [P, NT])
        w_raw = sb("w_raw", [P, 4, P])
        wT = sb("wT", [P, 4, P])
        wtq_row = sb("wtq_row", [2, P])
        wtqT = sb("wtqT", [P, 2])
        rows = sb("rows", [P, P])
        cols = sb("cols", [P, P])
        quant_cols = sb("quant_cols", [P, 3])
        wfq_raw = sb("wfq_raw", [P, 2])
        quant_w = sb("quant_w", [3, P])
        btq_bc = sb("btq_bc", [P, 2])
        br2_bc = sb("br2_bc", [P, E])
        wr1 = sb("wr1", [P, P])
        wr2 = sb("wr2", [P, E])
        b2z = sb("b2z", [P, NT, P])
        st6 = sb("st6", [P, NT, 6])
        mv = sb("mv", [P, NT, 2])
        ve = sb("ve", [P, NT])
        rstd = sb("rstd", [P, NT])
        xn = sb("xn", [P, NT, P])
        xnT = sb("xnT", [P, N])
        qT = sb("qT", [P, N])
        kT = sb("kT", [P, N])
        v_sb = sb("v_sb", [P, NT, P])
        qp = sb("qp", [P, NT, 2])
        a = sb("a", [P, NT, 2])
        mean2 = sb("mean2", [P, 2])
        sq = sb("sq", [P, NT, 2])
        nrm = sb("nrm", [P, NT])
        rn = sb("rn", [P, NT])
        r3 = sb("r3", [P, NT, 3])
        mom = sb("mom", [P, 4, NT])
        tot = sb("tot", [P, 4])
        sc = sb("sc", [P, 8])
        nay = sb("nay", [P, NT])
        ax12 = sb("ax12", [P, NT])
        lim = sb("lim", [P, NT])
        aT = sb("aT", [2, N])
        m2aT = sb("m2aT", [2, N])
        sqT = sb("sqT", [2, N])
        rT = sb("rT", [3, N])
        xbc = sb("xbc", [P, N])
        ybc = sb("ybc", [P, N])
        ady = sb("ady", [P, N])
        cone = sb("cone", [P, N], BF16)
        mask = sb("mask", [P, 2, N], BF16)
        nmax = sb("nmax", [P, NT])
        prob = sb("prob", [P, 2, N])
        rsum = sb("rsum", [P, NT])
        rinv = sb("rinv", [P, NT])
        probT = sb("probT", [P, NT, N])
        ctxT = sb("ctxT", [P, N])
        s_sb = sb("s_sb", [P, NT, P])
        xfT = sb("xfT", [P, N])
        r1T = sb("r1T", [P, N])
        lg = sb("lg", [P, NT, E])
        top8 = sb("top8", [P, NT, 8])
        idx8 = sb("idx8", [P, NT, 8], U32)
        idxf = sb("idxf", [P, NT, 8])
        dif = sb("dif", [P, NT, TOP])
        ew = sb("ew", [P, NT, TOP])
        esum = sb("esum", [P, NT])
        einv = sb("einv", [P, NT])
        hit = sb("hit", [P, NT * TOP, E])
        cpad = sb("cpad", [P, NT, EP])
        cT = sb("cT", [P, P])
        c_bc = [sb(f"c_bc{i}", [P, B * N]) for i in range(2)]
        w1_raw = sb("w1_raw", [P, FF])
        w2_raw = sb("w2_raw", [P, FC, P])
        w1_hi = [sb(f"w1_hi{i}", [P, FF], F32R) for i in range(2)]
        w1_lo = [sb(f"w1_lo{i}", [P, FF], F32R) for i in range(2)]
        w2_hi = [sb(f"w2_hi{i}", [P, FC, P], F32R) for i in range(2)]
        w2_lo = [sb(f"w2_lo{i}", [P, FC, P], F32R) for i in range(2)]
        g = sb("g", [P, FC, N])
        h_hi = sb("h_hi", [P, FC, N], F32R)
        h_lo = sb("h_lo", [P, FC, N], F32R)
        yc = sb("yc", [P, 2, N])

        def bank(name):
            return ctx.enter_context(nc.psum_tensor(name, [P, 512], F32))

        A0, A1, A2, A3 = [bank(f"A{i}") for i in range(4)]
        HB = [bank(f"HB{i}") for i in range(2)]
        YB = [bank(f"YB{i}") for i in range(2)]

        names = """consts_in pool_setup dve_setup pe_setup
            x_in pool_order dve_order act_order
            ln_stats rstd_ready xn_ready xnT_ps xnT_sb qp_ps q_ps k_ps v_ps q_sb k_sb v_sb_ready qp_sb mean_ps a_ready
            mom_ready mom_ps norm_ready rn_ready r3_ready var_ready std_ready aT_ps rT_ps aT_sb rT_sb xbc_ps ybc_ps
            xbc_sb ybc_sb dist_ps ady_ready mask_ready score_ps nmax_ready prob_ready probT_ps probT_sb ctx_ps ctx_sb
            o_ps s_ready xf_ready xfT_ps xfT_sb xsplit r1_ps r1_sb logit_ps logit_sb dif_ready ew_ready cpad_ready
            cT_ps cT_sb cT_stored init_ps acc_init
            w_in w_split c_in h_ps g_ready hi_ready split_ready chunk_read y_free y_done
            fin_copy fin_ps fin_stats fin_rstd fin_out stored dve_gate pool_gate sp_gate""".split()
        S = {n: sem(n) for n in names}

        block = ctx.enter_context(nc.Block())
        ROW = {"bq": 64, "bk": 65, "bv": 66, "bo": 67, "bfq": 68, "br1": 69}
        NROWS = 70

        def col(name):
            return cols[:, ROW[name]:ROW[name] + 1]

        def xb(tile, b):
            return tile[:, bass.ds(b * N, N)]

        def tiles(ap):
            return ap.rearrange("p (t d) -> p t d", t=NT)

        @block.sync
        def _(sp):
            n = 0

            def const(dst, src):
                nonlocal n
                sp.dma_start(dst, src).then_inc(S["consts_in"], 16)
                n += 1

            sp.dma_start(tiles(x_sb[:, 0:N]), x_d[0].rearrange("(t p) d -> p t d", p=P)).then_inc(S["x_in"], 16)
            for i, w in enumerate((Wq, Wk, Wv, Wo)):
                const(w_raw[:, i, :], w)
            const(wtq_row[:, :], Wtq)
            const(wfq_raw[:, :], Wfq)
            const(rows[0:E * FC, :], b1.rearrange("e (c p) -> (e c) p", p=P))
            for name, v in (("bq", bq), ("bk", bk), ("bv", bv), ("bo", bo), ("bfq", bfq), ("br1", br1)):
                const(rows[ROW[name]:ROW[name] + 1, :], v.rearrange("(o d) -> o d", o=1))
            const(btq_bc[:, :], btq.partition_broadcast(P))
            const(br2_bc[:, :], br2.partition_broadcast(P))
            const(wr1[:, :], Wr1)
            const(wr2[:, :], Wr2)
            sp.wait_ge(S["pool_setup"], POOL_B2Z)
            for t in range(NT):
                const(b2z[EP * t:EP * t + E, t, :], b2)
            assert n == NCONST

            with sp.Fori(0, B - 1) as b:
                sp.wait_ge(S["ln_stats"], 3 * b + 1)
                sp.dma_start(tiles(xb(x_sb, b + 1)), x_d[bass.ds(b + 1, 1)].rearrange("o (t p) d -> p (o t) d", p=P)
                             ).then_inc(S["x_in"], 16)
                sp.wait_ge(S["cT_sb"], b + 1)
                for t in range(NT):
                    sp.dma_start(cT_d[:, bass.ds(b * N + t * P, P)], cT[EP * t:EP * t + E, :]).then_inc(S["cT_stored"], 16)
            sp.wait_ge(S["cT_sb"], B)
            for t in range(NT):
                sp.dma_start(cT_d[:, (B - 1) * N + t * P:(B - 1) * N + (t + 1) * P],
                             cT[EP * t:EP * t + E, :]).then_inc(S["cT_stored"], 16)
            sp.wait_ge(S["cT_stored"], 16 * NT * B)

            def load_c(e, par):
                sp.dma_start(c_bc[par][:, :], cT_d[bass.ds(e, 1), :].broadcast_to([P, B * N])).then_inc(S["c_in"], 16)

            load_c(0, 0)
            sp.wait_ge(S["c_in"], 16)
            load_c(1, 1)
            with sp.Fori(1, E // 2) as e2:
                for par in range(2):
                    sp.wait_ge(S["y_done"], 16 * e2 + 8 * par - 8)
                    sp.sem_inc(S["sp_gate"], 1)
                    sp.wait_ge(S["c_in"], 32 * e2 + 16 * par)
                    sp.sem_inc(S["sp_gate"], 1)
                    load_c(2 * e2 + par, par)

            with sp.Fori(0, B) as b:
                sp.wait_ge(S["fin_out"], b + 1)
                sp.dma_start(out_d[bass.ds(b, 1)].rearrange("o (t p) d -> p (o t) d", p=P), tiles(xb(x_sb, b))
                             ).then_inc(S["stored"], 16)
            sp.wait_ge(S["stored"], 16 * B)

        @block.gpsimd
        def _(pool):
            order = 0

            def link(ins, name="pool_order"):
                nonlocal order
                order += 1
                ins.then_inc(S[name], 1)
                pool.wait_ge(S[name], order)

            link(pool.memset(b2z[:, :, :], 0.0), "pool_setup")
            assert order == POOL_B2Z
            link(pool.memset(ident[:, :], 0.0), "pool_setup")
            link(pool.memset(mask_w[:, :], 0.0), "pool_setup")
            link(pool.memset(tri[:, :], 0.0), "pool_setup")
            link(pool.memset(ones[:, :], 1.0), "pool_setup")
            link(pool.memset(avg[:, :], 1.0 / N), "pool_setup")
            link(pool.memset(half[:, :], 0.5), "pool_setup")
            link(pool.memset(mhalf[:, :], -0.5), "pool_setup")
            link(pool.memset(pick_x[:, :], 0.0), "pool_setup")
            link(pool.memset(pick_y[:, :], 1.0), "pool_setup")
            link(pool.memset(r3[:, :, :], 1.0), "pool_setup")
            link(pool.memset(cpad[:, :, :], 0.0), "pool_setup")
            link(pool.memset(pick_x[0:1, :], 1.0), "pool_setup")
            link(pool.memset(pick_y[0:1, :], 0.0), "pool_setup")
            link(pool.affine_select(out=ident[:, :], in_=ident[:, :], compare_op=ALU.not_equal, fill=1.0, base=0,
                                    pattern=[[-1, P]], channel_multiplier=1), "pool_setup")
            link(pool.affine_select(out=mask_w[:, :], in_=mask_w[:, :], compare_op=ALU.not_equal, fill=MASKED, base=0,
                                    pattern=[[-1, P]], channel_multiplier=1), "pool_setup")
            link(pool.affine_select(out=tri[:, :], in_=tri[:, :], compare_op=ALU.is_ge, fill=1.0, base=0,
                                    pattern=[[-1, P]], channel_multiplier=1), "pool_setup")
            link(pool.iota(iota_e[:, :], pattern=[[1, E]], base=0, channel_multiplier=0,
                           allow_small_or_imprecise_dtypes=True), "pool_setup")
            assert order == POOL_SETUP
            order = 0

            def own_wait():
                pool.sem_inc(S["pool_gate"], 1)

            def inverse_std(b, k, src_sem, src_val, dst_sem):
                pool.wait_ge(S[src_sem], src_val)
                own_wait()
                nc.gpsimd.tensor_scalar(ve[:, :], mv[:, :, 1], EPS, None, ALU.add).then_inc(S["pool_order"], 1)
                pool.wait_ge(S["pool_order"], k)
                nc.gpsimd.tensor_tensor(rstd[:, :], ve[:, :], mhalf[:, :], ALU.pow).then_inc(S[dst_sem], 1)

            with pool.Fori(0, B) as b:
                inverse_std(b, 3 * b + 1, "ln_stats", 3 * b + 1, "rstd_ready")
                pool.wait_ge(S["norm_ready"], b + 1)
                nc.gpsimd.tensor_tensor(rn[:, :], nrm[:, :], mhalf[:, :], ALU.pow).then_inc(S["rn_ready"], 1)
                pool.wait_ge(S["var_ready"], b + 1)
                nc.gpsimd.tensor_tensor(sc[:, 6:7], sc[:, 5:6], half[:, 0:1], ALU.pow).then_inc(S["std_ready"], 1)
                inverse_std(b, 3 * b + 2, "ln_stats", 3 * b + 2, "rstd_ready")
                inverse_std(b, 3 * b + 3, "ln_stats", 3 * b + 3, "rstd_ready")

            def split(e, par):
                pool.dma_start(w1_raw[:, :], W1[bass.ds(e, 1)].rearrange("o h f -> h (o f)")).then_inc(S["w_in"], 16)
                pool.dma_start(w2_raw[:, :, :], W2[bass.ds(e, 1)].rearrange("o (c p) h -> p (o c) h", p=P)
                               ).then_inc(S["w_in"], 16)
                pool.wait_ge(S["w_in"], 32 * e + 32)
                own_wait()
                nc.gpsimd.tensor_copy(w1_hi[par][:, :], w1_raw[:, :])
                nc.gpsimd.tensor_copy(w2_hi[par][:, :, :], w2_raw[:, :, :]).then_inc(S["pool_order"], 1)
                pool.wait_ge(S["pool_order"], 3 * B + e + 1)
                nc.gpsimd.tensor_tensor(w1_lo[par][:, :], w1_raw[:, :], w1_hi[par][:, :].bitcast(F32), ALU.subtract)
                nc.gpsimd.tensor_tensor(w2_lo[par][:, :, :], w2_raw[:, :, :], w2_hi[par][:, :, :].bitcast(F32),
                                        ALU.subtract).then_inc(S["w_split"], 1)
                pool.wait_ge(S["w_split"], e + 1)

            split(0, 0)
            split(1, 1)
            with pool.Fori(0, E // 2 - 1) as e2:
                for par in range(2):
                    pool.wait_ge(S["chunk_read"], FC * B * (2 * e2 + par + 1))
                    split(2 * e2 + par + 2, par)

            with pool.Fori(0, B) as b:
                inverse_std(b, 3 * B + E + 1 + b, "fin_stats", b + 1, "fin_rstd")

        @block.vector
        def _(dve):
            V = nc.vector
            dve.wait_ge(S["consts_in"], 16 * NCONST)
            dve.wait_ge(S["pool_setup"], POOL_SETUP)
            n = 0

            def setup(ins):
                nonlocal n
                n += 1
                ins.then_inc(S["dve_setup"], 1)

            dve.wait_ge(S["pe_setup"], 1)
            setup(V.tensor_copy(wT[:, :, :].rearrange("p a d -> p (a d)"), A0[:, :]))
            setup(V.tensor_copy(wtqT[:, :], A1[:, 0:2]))
            setup(V.tensor_copy(cols[:, 0:NROWS], A1[:, P:P + NROWS]))
            dve.wait_ge(S["dve_setup"], 3)
            setup(V.tensor_scalar(quant_cols[:, 0:2], wfq_raw[:, :], QUANTUM, None, ALU.mult))
            dve.wait_ge(S["pe_setup"], 2)
            setup(V.tensor_tensor(quant_cols[:, 2:3], A2[:, 0:1], col("bo"), ALU.add))
            dve.wait_ge(S["dve_setup"], 5)
            setup(V.scalar_tensor_tensor(quant_cols[:, 2:3], col("bfq"), QUANTUM, quant_cols[:, 2:3], ALU.mult, ALU.add))
            dve.wait_ge(S["pe_setup"], 3)
            setup(V.tensor_copy(quant_w[:, :], A3[0:3, 0:P]))
            assert n == DVE_SETUP

            def own_wait():
                dve.sem_inc(S["dve_gate"], 1)

            class Order:
                def __init__(self, base, per):
                    self.base, self.per, self.n = base, per, 0

                def __call__(self, ins):
                    self.n += 1
                    ins.then_inc(S["dve_order"], 1)
                    dve.wait_ge(S["dve_order"], self.base + self.n)

            def stats(src):
                for t in range(NT):
                    last = V.bn_stats(st6[:, t, :], src[:, t, :])
                return last

            def aggregate():
                own_wait()
                for t in range(NT):
                    last = V.bn_aggr(mv[:, t, :], st6[:, t, :])
                return last

            def normalise(dst, src):
                for t in range(NT):
                    last = V.tensor_scalar(dst[:, t, :], src[:, t, :], mv[:, t, 0:1], rstd[:, t:t + 1],
                                           ALU.subtract, ALU.mult)
                return last

            def attention(b, first=False):
                link = Order(b * DVE_ORDER, DVE_ORDER)
                x = tiles(xb(x_sb, b))
                dve.wait_ge(S["x_in"], 16 * b + 16)
                own_wait()
                link(stats(x))
                aggregate().then_inc(S["ln_stats"], 1)
                dve.wait_ge(S["rstd_ready"], 3 * b + 1)
                normalise(xn, x).then_inc(S["xn_ready"], 1)
                dve.wait_ge(S["qp_ps"], b + 1)
                V.tensor_tensor(qp[:, :, :], A0[:, 0:2 * NT].rearrange("p (t c) -> p t c", c=2),
                                btq_bc[:, :].unsqueeze(1).broadcast_to([P, NT, 2]), ALU.add).then_inc(S["qp_sb"], 1)
                dve.wait_ge(S["qp_sb"], b + 1)
                link(V.tensor_tensor(sq[:, :, :], qp[:, :, :], qp[:, :, :], ALU.mult))
                link(V.tensor_tensor(nrm[:, :], sq[:, :, 0], sq[:, :, 1], ALU.add))
                V.tensor_scalar(nrm[:, :], nrm[:, :], TINY_NORM ** 2, None, ALU.max).then_inc(S["norm_ready"], 1)
                dve.wait_ge(S["mean_ps"], b + 1)
                link(V.tensor_reduce(mean2[:, :], A0[:, 2 * NT:4 * NT].rearrange("p (t c) -> p c t", c=2),
                                     AX_X, ALU.add))
                V.tensor_tensor(a[:, :, :], qp[:, :, :], mean2[:, :].unsqueeze(1).broadcast_to([P, NT, 2]),
                                ALU.subtract).then_inc(S["a_ready"], 1)
                dve.wait_ge(S["a_ready"], b + 1)
                V.tensor_tensor(mom[:, 0, :], a[:, :, 0], a[:, :, 0], ALU.mult)
                V.tensor_tensor(mom[:, 1, :], a[:, :, 1], a[:, :, 1], ALU.mult)
                link(V.tensor_tensor(mom[:, 2, :], a[:, :, 0], a[:, :, 1], ALU.mult))
                dve.wait_ge(S["rn_ready"], b + 1)
                link(V.tensor_tensor(nrm[:, :], mom[:, 0, :], mom[:, 1, :], ALU.add))
                V.tensor_tensor(mom[:, 3, :], nrm[:, :], nrm[:, :], ALU.mult).then_inc(S["mom_ready"], 1)
                V.tensor_tensor(r3[:, :, 0:2], qp[:, :, :], rn[:, :].unsqueeze(2).broadcast_to([P, NT, 2]),
                                ALU.mult).then_inc(S["r3_ready"], 1)
                V.tensor_scalar(nay[:, :], a[:, :, 1], -1.0, None, ALU.mult)
                V.tensor_scalar(ax12[:, :], a[:, :, 0], PI_CONE, None, ALU.mult)
                dve.wait_ge(S["k_ps"], b + 1)
                V.tensor_scalar(kT[:, :], A2[:, :], col("bk"), SCALE, ALU.add, ALU.mult).then_inc(S["k_sb"], 1)
                dve.wait_ge(S["mom_ps"], b + 1)
                link(V.tensor_reduce(tot[:, :], A0[:, 4 * NT:8 * NT].rearrange("p (q t) -> p q t", t=NT), AX_X, ALU.add))
                sxx, syy, sxy, snn = (tot[:, i:i + 1] for i in range(4))
                link(V.tensor_tensor(sc[:, 0:1], sxx, syy, ALU.add))
                link(V.scalar_tensor_tensor(sc[:, 1:2], sc[:, 0:1], -0.5, sc[:, 0:1], ALU.mult, ALU.mult))
                link(V.scalar_tensor_tensor(sc[:, 1:2], snn, N / 2.0, sc[:, 1:2], ALU.mult, ALU.add))
                link(V.scalar_tensor_tensor(sc[:, 2:3], sxx, sxx, sc[:, 1:2], ALU.mult, ALU.add))
                link(V.scalar_tensor_tensor(sc[:, 3:4], syy, syy, sc[:, 2:3], ALU.mult, ALU.add))
                link(V.tensor_tensor(sc[:, 4:5], sxy, sxy, ALU.mult))
                link(V.scalar_tensor_tensor(sc[:, 4:5], sc[:, 4:5], 2.0, sc[:, 3:4], ALU.mult, ALU.add))
                V.tensor_scalar(sc[:, 5:6], sc[:, 4:5], 4.0 / (PAIRS - 1.0), 0.0, ALU.mult, ALU.max
                                ).then_inc(S["var_ready"], 1)
                dve.wait_ge(S["std_ready"], b + 1)
                link(V.tensor_scalar(sc[:, 7:8], sc[:, 6:7], THRESHOLD_FACTOR, None, ALU.mult))
                link(V.scalar_tensor_tensor(sc[:, 7:8], sc[:, 0:1], 2.0 / N, sc[:, 7:8], ALU.mult, ALU.add))
                link(V.tensor_scalar(lim[:, :], nrm[:, :], -1.0, sc[:, 7:8], ALU.mult, ALU.add))
                for t in range(NT):
                    w = P * (t + 1)
                    dve.wait_ge(S["ady_ready"], NT * b + t + 1)
                    link(V.scalar_tensor_tensor(cone[:, 0:w], xbc[:, 0:w], ax12[:, t:t + 1], ady[:, 0:w],
                                                ALU.subtract, ALU.is_gt))
                    dve.wait_ge(S["dist_ps"], NT * b + t + 1)
                    if t >= 2:
                        dve.wait_ge(S["score_ps"], NT * b + t - 1)
                    V.scalar_tensor_tensor(mask[:, t % 2, 0:w], A3[:, 0:w], lim[:, t:t + 1], cone[:, 0:w],
                                           ALU.is_gt, ALU.max).then_inc(S["mask_ready"], 1)
                    dve.wait_ge(S["score_ps"], NT * b + t + 1)
                    V.tensor_reduce(nmax[:, t:t + 1], (A1, A0)[t % 2][:, 0:w], AX_X, ALU.max, negate=True
                                    ).then_inc(S["nmax_ready"], 1)
                dve.wait_ge(S["prob_ready"], NT * (b + 1))
                link(V.reciprocal(rinv[:, :], rsum[:, :]))
                dve.wait_ge(S["o_ps"], b + 1)
                for t in range(NT):
                    last = V.scalar_tensor_tensor(s_sb[:, t, :], A0[:, t * P:(t + 1) * P], rinv[:, t:t + 1], xn[:, t, :],
                                                  ALU.mult, ALU.add)
                link(last)
                V.tensor_tensor(s_sb[:, :, :], tiles(A1[:, :]), s_sb[:, :, :], ALU.add).then_inc(S["s_ready"], 1)
                dve.wait_ge(S["s_ready"], b + 1)
                own_wait()
                link(stats(s_sb))
                aggregate().then_inc(S["ln_stats"], 1)
                dve.wait_ge(S["rstd_ready"], 3 * b + 2)
                link(normalise(s_sb, s_sb))
                link(V.tensor_tensor(x, x, s_sb[:, :, :], ALU.add))
                own_wait()
                link(stats(x))
                aggregate().then_inc(S["ln_stats"], 1)
                dve.wait_ge(S["rstd_ready"], 3 * b + 3)
                normalise(s_sb, x).then_inc(S["xf_ready"], 1)
                dve.wait_ge(S["xfT_sb"], b + 1)
                link(V.tensor_copy(xb(x_hi, b), xfT[:, :]))
                V.tensor_tensor(xb(x_lo, b), xfT[:, :], xb(x_hi, b).bitcast(F32), ALU.subtract).then_inc(S["xsplit"], 1)
                dve.wait_ge(S["logit_ps"], b + 1)
                V.tensor_tensor(lg[:, :, :], A0[:, 0:NT * E].rearrange("p (t e) -> p t e", e=E),
                                br2_bc[:, :].unsqueeze(1).broadcast_to([P, NT, E]), ALU.add).then_inc(S["logit_sb"], 1)
                dve.wait_ge(S["logit_sb"], b + 1)
                own_wait()
                for t in range(NT):
                    last = V.max(top8[:, t, :], lg[:, t, :])
                link(last)
                own_wait()
                for t in range(NT):
                    V.max_index(idx8[:, t, :], top8[:, t, :], lg[:, t, :])
                V.tensor_tensor(dif[:, :, :], top8[:, :, 0:TOP], top8[:, :, 0:1].broadcast_to([P, NT, TOP]), ALU.subtract
                                ).then_inc(S["dif_ready"], 1)
                dve.wait_ge(S["dif_ready"], b + 1)
                link(V.tensor_copy(idxf[:, :, :], idx8[:, :, :]))
                h4 = hit[:, :, :].rearrange("p (t k) e -> p t k e", k=TOP)
                for t in range(NT):
                    last = V.tensor_tensor(h4[:, t], idxf[:, t, 0:TOP].unsqueeze(2).broadcast_to([P, TOP, E]),
                                           iota_e[:, :].unsqueeze(1).broadcast_to([P, TOP, E]), ALU.is_equal)
                link(last)
                dve.wait_ge(S["ew_ready"], b + 1)
                link(V.tensor_reduce(esum[:, :], ew[:, :, :], AX_X, ALU.add))
                link(V.reciprocal(einv[:, :], esum[:, :]))
                link(V.tensor_tensor(ew[:, :, :], ew[:, :, :], einv[:, :].unsqueeze(2).broadcast_to([P, NT, TOP]),
                                     ALU.mult))
                link(V.tensor_tensor(hit[:, :, :], hit[:, :, :],
                                     ew[:, :, :].rearrange("p t k -> p (t k)").unsqueeze(2).broadcast_to([P, NT * TOP, E]),
                                     ALU.mult))
                V.tensor_reduce(cpad[:, :, 0:E], hit[:, :, :].rearrange("p (t k) e -> p t e k", k=TOP), AX_X, ALU.add
                                ).then_inc(S["cpad_ready"], 1)
                dve.wait_ge(S["cT_ps"], b + 1)
                if not first:
                    dve.wait_ge(S["cT_stored"], 16 * NT * b)
                V.tensor_copy(cT[:, :], A1[:, 0:P]).then_inc(S["cT_sb"], 1)
                dve.wait_ge(S["init_ps"], b + 1)
                V.tensor_copy(xb(acc, b), A2[:, :]).then_inc(S["acc_init"], 1)
                assert link.n == DVE_ORDER, link.n

            attention(0, True)
            with dve.Fori(1, B) as b:
                attention(b)

            base = B * DVE_ORDER

            def split_hidden(u, first=False):
                for c in range(FC):
                    dve.wait_ge(S["g_ready"], FC * u + c + 1)
                    if not first:
                        dve.wait_ge(S["chunk_read"], FC * (u - 1) + c + 1)
                    if c % 2 == 1:
                        V.tensor_copy(h_hi[:, c, :], g[:, c, :]).then_inc(S["hi_ready"], 1)
                        dve.wait_ge(S["hi_ready"], 2 * u + c // 2 + 1)
                    V.tensor_tensor(h_lo[:, c, :], g[:, c, :], h_hi[:, c, :].bitcast(F32), ALU.subtract
                                    ).then_inc(S["split_ready"], 1)

            def accumulate(u, b, ypar, cpar):
                dve.wait_ge(S["chunk_read"], FC * (u + 1))
                V.tensor_tensor(yc[:, ypar, :], YB[ypar][:, :], xb(c_bc[cpar], b), ALU.mult).then_inc(S["y_free"], 1)
                dve.wait_ge(S["y_free"], 2 + u + 1)
                V.tensor_tensor(xb(acc, b), xb(acc, b), yc[:, ypar, :], ALU.add).then_inc(S["y_done"], 1)

            def expert(e, par, first=False):
                split_hidden(8 * e, first)
                if not first:
                    accumulate(8 * e - 1, B - 1, 1, 1 - par)
                dve.wait_ge(S["c_in"], 16 * e + 16)
                own_wait()
                with dve.Fori(0, B // 2 - 1) as i:
                    for k in range(2):
                        split_hidden(8 * e + 2 * i + k + 1)
                        accumulate(8 * e + 2 * i + k, 2 * i + k, k, par)
                split_hidden(8 * e + 7)
                accumulate(8 * e + 6, B - 2, 0, par)

            dve.sem_inc(S["y_free"], 2)
            expert(0, 0, True)
            expert(1, 1)
            with dve.Fori(1, E // 2) as e2:
                expert(2 * e2, 0)
                expert(2 * e2 + 1, 1)
            accumulate(8 * E - 1, B - 1, 1, 1)

            fb = base
            with dve.Fori(0, B // 2) as b2i:
                for k in range(2):
                    b = 2 * b2i + k
                    f = tiles((A0, A1)[k][:, :])
                    dve.wait_ge(S["fin_ps"], b + 1)
                    own_wait()
                    stats(f).then_inc(S["dve_order"], 1)
                    dve.wait_ge(S["dve_order"], fb + 2 * b + 1)
                    aggregate().then_inc(S["fin_stats"], 1)
                    dve.wait_ge(S["fin_rstd"], b + 1)
                    normalise(s_sb, f).then_inc(S["dve_order"], 1)
                    dve.wait_ge(S["dve_order"], fb + 2 * b + 2)
                    x = tiles(xb(x_sb, b))
                    V.tensor_tensor(x, x, s_sb[:, :, :], ALU.add).then_inc(S["fin_out"], 1)
                    dve.wait_ge(S["fin_out"], b + 1)

        @block.scalar
        def _(act):
            A = nc.scalar
            act.wait_ge(S["dve_setup"], DVE_SETUP)

            def attention(b):
                act.wait_ge(S["xnT_ps"], b + 1)
                A.copy(xnT[:, :], A0[:, :]).then_inc(S["xnT_sb"], 1)
                act.wait_ge(S["q_ps"], b + 1)
                A.activation(qT[:, :], A1[:, :], ACT.Identity, bias=col("bq")).then_inc(S["q_sb"], 1)
                act.wait_ge(S["v_ps"], b + 1)
                A.copy(v_sb[:, :, :].rearrange("p t d -> p (t d)"), A3[:, :]).then_inc(S["v_sb_ready"], 1)
                act.wait_ge(S["aT_ps"], b + 1)
                A.copy(aT[:, :], A1[0:2, :])
                A.mul(m2aT[:, :], A1[0:2, :], -2.0)
                A.activation(sqT[:, :], A1[0:2, :], ACT.Square).then_inc(S["aT_sb"], 1)
                act.wait_ge(S["rT_ps"], b + 1)
                A.copy(rT[:, :], A2[0:3, :]).then_inc(S["rT_sb"], 1)
                act.wait_ge(S["xbc_ps"], b + 1)
                A.mul(xbc[:, :], A1[:, :], PI_CONE).then_inc(S["xbc_sb"], 1)
                act.wait_ge(S["ybc_ps"], b + 1)
                A.copy(ybc[:, :], A2[:, :]).then_inc(S["ybc_sb"], 1)
                act.wait_ge(S["ybc_sb"], b + 1)

                def abs_dy(t):
                    w = P * (t + 1)
                    if t >= 1:
                        act.wait_ge(S["mask_ready"], NT * b + t)
                    else:
                        act.wait_ge(S["r3_ready"], b + 1)
                    A.activation(ady[:, 0:w], ybc[:, 0:w], ACT.Abs, bias=nay[:, t:t + 1]).then_inc(S["ady_ready"], 1)

                def softmax(t):
                    w = P * (t + 1)
                    act.wait_ge(S["nmax_ready"], NT * b + t + 1)
                    if t >= 2:
                        act.wait_ge(S["probT_ps"], NT * b + t - 1)
                    A.activation(prob[:, t % 2, 0:w], (A1, A0)[t % 2][:, 0:w], ACT.Exp, bias=nmax[:, t:t + 1],
                                 accum_out=rsum[:, t:t + 1]).then_inc(S["prob_ready"], 1)

                def transposed(t):
                    act.wait_ge(S["probT_ps"], NT * b + t + 1)
                    A.copy(probT[:, 0:t + 1, t * P:(t + 1) * P], A2[:, 0:P * (t + 1)].rearrange("p (j i) -> p j i", i=P)
                           ).then_inc(S["probT_sb"], 1)

                act.wait_ge(S["k_sb"], b + 1)
                abs_dy(0)
                for t in range(NT):
                    softmax(t)
                    if t + 1 < NT:
                        abs_dy(t + 1)
                    transposed(t)
                act.wait_ge(S["ctx_ps"], b + 1)
                A.copy(ctxT[:, :], A3[:, :]).then_inc(S["ctx_sb"], 1)
                act.wait_ge(S["xfT_ps"], b + 1)
                A.copy(xfT[:, :], A2[:, :]).then_inc(S["xfT_sb"], 1)
                act.wait_ge(S["r1_ps"], b + 1)
                A.activation(r1T[:, :], A3[:, :], ACT.Relu, bias=col("br1")).then_inc(S["r1_sb"], 1)
                act.wait_ge(S["dif_ready"], b + 1)
                A.activation(ew[:, :, :], dif[:, :, :], ACT.Exp).then_inc(S["ew_ready"], 1)

            with act.Fori(0, B) as b:
                attention(b)

            def hidden(u, e, first=False):
                for c in range(FC):
                    act.wait_ge(S["h_ps"], FC * u + c + 1)
                    if not first:
                        act.wait_ge(S["split_ready"], FC * (u - 1) + c + 1)
                        act.wait_ge(S["chunk_read"], FC * (u - 1) + c + 1)
                    bias = cols[:, bass.ds(FC * e + c, 1)]
                    if c % 2 == 0:
                        A.activation(h_hi[:, c, :], HB[c % 2][:, :], ACT.Gelu, bias=bias)
                    A.activation(g[:, c, :], HB[c % 2][:, :], ACT.Gelu, bias=bias).then_inc(S["g_ready"], 1)

            hidden(0, 0, True)
            with act.Fori(1, B) as b:
                hidden(b, 0)
            with act.Fori(1, E) as e:
                with act.Fori(0, B) as b:
                    hidden(8 * e + b, e)

            act.wait_ge(S["y_done"], 8 * E)
            A.copy(xfT[:, :], acc[:, 0:N]).then_inc(S["fin_copy"], 1)
            with act.Fori(1, B) as b:
                act.wait_ge(S["fin_ps"], b)
                A.copy(xfT[:, :], xb(acc, b)).then_inc(S["fin_copy"], 1)

        @block.tensor
        def _(pe):
            T = nc.tensor
            pe.wait_ge(S["consts_in"], 16 * NCONST)
            pe.wait_ge(S["pool_setup"], POOL_SETUP)
            for i in range(4):
                T.transpose(A0[:, i * P:(i + 1) * P], w_raw[:, i, :], ident[:, :])
            T.transpose(A1[:, 0:2], wtq_row[:, :], ident[0:2, 0:2])
            T.transpose(A1[:, P:P + NROWS], rows[0:NROWS, :], ident[0:NROWS, 0:NROWS]).then_inc(S["pe_setup"], 1)
            pe.wait_ge(S["dve_setup"], 3)
            T.matmul(A2[:, 0:1], wT[:, 3, :], col("bv"), start=True, stop=True).then_inc(S["pe_setup"], 1)
            pe.wait_ge(S["dve_setup"], 6)
            T.transpose(A3[0:3, 0:P], quant_cols[:, :], ident[:, :]).then_inc(S["pe_setup"], 1)
            pe.wait_ge(S["dve_setup"], DVE_SETUP)

            def attention(b, first=False):
                def ts(t):
                    return slice(t * P, (t + 1) * P)

                pe.wait_ge(S["xn_ready"], b + 1)
                if not first:
                    pe.wait_ge(S["logit_sb"], b)
                for t in range(NT):
                    last = T.transpose(A0[:, ts(t)], xn[:, t, :], ident[:, :])
                last.then_inc(S["xnT_ps"], 1)
                pe.wait_ge(S["xnT_sb"], b + 1)
                for t in range(NT):
                    last = T.matmul(A0[:, 2 * t:2 * t + 2], xnT[:, ts(t)], wtqT[:, :], start=True, stop=True)
                last.then_inc(S["qp_ps"], 1)
                if not first:
                    pe.wait_ge(S["cT_sb"], b)
                T.matmul(A1[:, :], wT[:, 0, :], xnT[:, :], start=True, stop=True).then_inc(S["q_ps"], 1)
                pe.wait_ge(S["qp_sb"], b + 1)
                T.matmul(A0[:, 2 * NT:4 * NT], avg[:, :], qp[:, :, :].rearrange("p t c -> p (t c)"),
                         start=True, stop=True).then_inc(S["mean_ps"], 1)
                if not first:
                    pe.wait_ge(S["acc_init"], b)
                T.matmul(A2[:, :], wT[:, 1, :], xnT[:, :], start=True, stop=True).then_inc(S["k_ps"], 1)
                for t in range(NT):
                    last = T.matmul(A3[:, ts(t)], xnT[:, ts(t)], wT[:, 2, :], start=True, stop=True)
                last.then_inc(S["v_ps"], 1)
                pe.wait_ge(S["a_ready"], b + 1)
                pe.wait_ge(S["q_sb"], b + 1)
                for t in range(NT):
                    last = T.transpose(A1[0:2, ts(t)], a[:, t, :], ident[:, :])
                last.then_inc(S["aT_ps"], 1)
                pe.wait_ge(S["mom_ready"], b + 1)
                T.matmul(A0[:, 4 * NT:8 * NT], ones[:, :], mom[:, :, :].rearrange("p q t -> p (q t)"),
                         start=True, stop=True).then_inc(S["mom_ps"], 1)
                pe.wait_ge(S["r3_ready"], b + 1)
                pe.wait_ge(S["k_sb"], b + 1)
                for t in range(NT):
                    last = T.transpose(A2[0:3, ts(t)], r3[:, t, :], ident[:, :])
                last.then_inc(S["rT_ps"], 1)
                pe.wait_ge(S["aT_sb"], b + 1)
                T.matmul(A1[:, :], pick_x[:, :], aT[:, :], start=True, stop=True).then_inc(S["xbc_ps"], 1)
                pe.wait_ge(S["rT_sb"], b + 1)
                T.matmul(A2[:, :], pick_y[:, :], aT[:, :], start=True, stop=True).then_inc(S["ybc_ps"], 1)
                pe.wait_ge(S["v_sb_ready"], b + 1)

                def distance(t):
                    w = P * (t + 1)
                    if t >= 1:
                        pe.wait_ge(S["mask_ready"], NT * b + t)
                    T.matmul(A3[:, 0:w], m2aT[:, ts(t)], aT[:, 0:w], start=True, stop=False)
                    T.matmul(A3[:, 0:w], ones[0:2, :], sqT[:, 0:w], start=False, stop=True).then_inc(S["dist_ps"], 1)

                def transpose_prob(t):
                    pe.wait_ge(S["prob_ready"], NT * b + t + 1)
                    if t >= 1:
                        pe.wait_ge(S["probT_sb"], NT * b + t)
                    else:
                        pe.wait_ge(S["ybc_sb"], b + 1)
                    for j in range(t + 1):
                        last = T.transpose(A2[:, ts(j)], prob[:, t % 2, ts(j)], ident[:, :])
                    last.then_inc(S["probT_ps"], 1)

                distance(0)
                for t in range(NT):
                    w = P * (t + 1)
                    s = (A1, A0)[t % 2]
                    if t == 0:
                        pe.wait_ge(S["xbc_sb"], b + 1)
                    elif t == 1:
                        pe.wait_ge(S["std_ready"], b + 1)
                    else:
                        pe.wait_ge(S["prob_ready"], NT * b + t - 1)
                    T.matmul(s[:, 0:w], qT[:, ts(t)], kT[:, 0:w], start=True, stop=False)
                    T.matmul(s[:, ts(t)], mask_w[:, :], tri[:, :], start=False, stop=False)
                    pe.wait_ge(S["mask_ready"], NT * b + t + 1)
                    T.matmul(s[:, 0:w], mask_w[:, :], mask[:, t % 2, 0:w], start=False, stop=True
                             ).then_inc(S["score_ps"], 1)
                    if t + 1 < NT:
                        distance(t + 1)
                    if t >= 1:
                        transpose_prob(t - 1)
                transpose_prob(NT - 1)
                pe.wait_ge(S["probT_sb"], NT * (b + 1))
                for j in range(NT):
                    last = T.matmul(A3[:, j * P:N], v_sb[:, j, :], probT[:, j, j * P:N], start=(j == 0), stop=(j == NT - 1))
                last.then_inc(S["ctx_ps"], 1)
                for t in range(NT):
                    T.matmul(A1[:, ts(t)], rT[:, ts(t)], quant_w[:, :], start=True, stop=True)
                pe.wait_ge(S["ctx_sb"], b + 1)
                for t in range(NT):
                    last = T.matmul(A0[:, ts(t)], ctxT[:, ts(t)], wT[:, 3, :], start=True, stop=True)
                last.then_inc(S["o_ps"], 1)
                pe.wait_ge(S["xf_ready"], b + 1)
                for t in range(NT):
                    last = T.transpose(A2[:, ts(t)], s_sb[:, t, :], ident[:, :])
                last.then_inc(S["xfT_ps"], 1)
                pe.wait_ge(S["xfT_sb"], b + 1)
                T.matmul(A3[:, :], wr1[:, :], xfT[:, :], start=True, stop=True).then_inc(S["r1_ps"], 1)
                pe.wait_ge(S["r1_sb"], b + 1)
                for t in range(NT):
                    last = T.matmul(A0[:, t * E:(t + 1) * E], r1T[:, ts(t)], wr2[:, :], start=True, stop=True)
                last.then_inc(S["logit_ps"], 1)
                pe.wait_ge(S["cpad_ready"], b + 1)
                T.transpose(A1[:, 0:P], cpad[:, :, :].rearrange("p t e -> p (t e)"), ident[:, :]).then_inc(S["cT_ps"], 1)
                pe.wait_ge(S["cT_sb"], b + 1)
                for t in range(NT):
                    last = T.matmul(A2[:, ts(t)], b2z[:, t, :], cT[:, :], start=True, stop=True)
                last.then_inc(S["init_ps"], 1)

            attention(0, True)
            with pe.Fori(1, B) as b:
                attention(b)

            def up(u, b, c, par, first=False):
                if not (first and c < 2):
                    pe.wait_ge(S["g_ready"], FC * u + c - 1)
                w = slice(c * P, (c + 1) * P)
                T.matmul(HB[c % 2][:, :], w1_hi[par][:, w], xb(x_hi, b), start=True, stop=False)
                T.matmul(HB[c % 2][:, :], w1_hi[par][:, w], xb(x_lo, b), start=False, stop=False)
                T.matmul(HB[c % 2][:, :], w1_lo[par][:, w], xb(x_hi, b), start=False, stop=True).then_inc(S["h_ps"], 1)

            def down(u, c, par, ypar):
                pe.wait_ge(S["split_ready"], FC * u + c + 1)
                if c == 0:
                    pe.wait_ge(S["y_free"], u + 1)
                y = YB[ypar]
                T.matmul(y[:, :], w2_hi[par][:, c, :], h_hi[:, c, :], start=(c == 0), stop=False)
                T.matmul(y[:, :], w2_lo[par][:, c, :], h_hi[:, c, :], start=False, stop=False)
                T.matmul(y[:, :], w2_hi[par][:, c, :], h_lo[:, c, :], start=False, stop=(c == FC - 1)
                         ).then_inc(S["chunk_read"], 1)

            def expert(e, par, first=False):
                pe.wait_ge(S["w_split"], e + 1)
                for c in range(FC):
                    up(8 * e, 0, c, par, first)
                    if not first:
                        down(8 * e - 1, c, 1 - par, 1)
                with pe.Fori(0, B // 2 - 1) as i:
                    for k in range(2):
                        for c in range(FC):
                            up(8 * e + 2 * i + k + 1, 2 * i + k + 1, c, par)
                            down(8 * e + 2 * i + k, c, par, k)
                for c in range(FC):
                    up(8 * e + 7, B - 1, c, par)
                    down(8 * e + 6, c, par, 0)

            pe.wait_ge(S["xsplit"], B)
            expert(0, 0, True)
            expert(1, 1)
            with pe.Fori(1, E // 2) as e2:
                expert(2 * e2, 0)
                expert(2 * e2 + 1, 1)
            for c in range(FC):
                down(8 * E - 1, c, 1, 1)

            def final(b, k):
                pe.wait_ge(S["fin_copy"], b + 1)
                for t in range(NT):
                    last = T.transpose((A0, A1)[k][:, t * P:(t + 1) * P], xfT[:, t * P:(t + 1) * P], ident[:, :])
                last.then_inc(S["fin_ps"], 1)

            final(0, 0)
            final(1, 1)
            with pe.Fori(1, B // 2) as b2i:
                for k in range(2):
                    pe.wait_ge(S["fin_out"], 2 * b2i + k - 1)
                    final(2 * b2i + k, k)


POOL_B2Z = 1
POOL_SETUP = 18
DVE_SETUP = 7
DVE_ORDER = 35
NCONST = 4 + 1 + 1 + 1 + 6 + 2 + 2 + 4

_INS = ["L0_attn_hidden_states", "L0_attn_Wq", "L0_attn_bq", "L0_attn_Wk", "L0_attn_bk", "L0_attn_Wv", "L0_attn_bv",
        "L0_attn_Wo", "L0_attn_bo", "L0_attn_Wtq", "L0_attn_btq", "L0_attn_Wfq", "L0_attn_bfq",
        "L0_ffn_Wr1", "L0_ffn_br1", "L0_ffn_Wr2", "L0_ffn_br2", "L0_ffn_W1", "L0_ffn_b1", "L0_ffn_W2", "L0_ffn_b2"]


def kernel(**inputs):
    import numpy as _np
    import concourse.bacc as _bacc
    from concourse import mybir as _mybir
    from concourse.bass_utils import run_bass_kernel_spmd as _run

    nc = _bacc.Bacc("TRN2", target_bir_lowering=False, num_devices=1)
    arrays, args = {}, []
    for name in _INS:
        a = _np.ascontiguousarray(inputs[name])
        arrays[f"in_{name}_dram"] = a
        args.append(nc.dram_tensor(f"in_{name}_dram", a.shape, _mybir.dt.from_np(a.dtype), kind="ExternalInput").ap())
    shape = inputs[_INS[0]].shape
    args.append(nc.dram_tensor("out_0_dram", tuple(shape), _mybir.dt.float32, kind="ExternalOutput").ap())
    attention_moe_kernel(nc, *args)
    r = _run(nc, [arrays], core_ids=[0])
    return r.results[0]["out_0_dram"]
```

```python
from contextlib import ExitStack

import concourse.bass as bass
from concourse import mybir

F32 = mybir.dt.float32
F32R = mybir.dt.float32r
BF16 = mybir.dt.bfloat16
U32 = mybir.dt.uint32
ALU = mybir.AluOpType
ACT = mybir.ActivationFunctionType
AX_X = mybir.AxisListType.X


P = 128
EPS = 1e-5
TINY_NORM = 1e-12
THRESHOLD_FACTOR = 1.25
QUANTUM = 0.1
PI_CONE = 2.0 ** -12
MASKED = -(2.0 ** 40)
EULER = 2.718281828459045
TOP = 4
CHUNK_LAG = 4
SCALAR_HALVES = (0, 2)


def attention_moe_kernel(nc, x_d, Wq, bq, Wk, bk, Wv, bv, Wo, bo, Wtq, btq, Wfq, bfq,
                         Wr1, br1, Wr2, br2, W1, b1, W2, b2, out_d):
    B, N, D = x_d.shape
    E, _, FF = W1.shape
    NT = N // P
    FC = FF // P
    SLOTS = E * FC
    assert D == P and N == 512 and FC == 4 and E == 16 and CHUNK_LAG == FC
    SCALE = float(D) ** -0.5
    PAIRS = float(N) * float(N)

    cT_d = nc.dram_tensor("routing_scratch", (E, B * N), F32, kind="Internal").ap()

    ctx = ExitStack()
    with ctx:
        def sb(name, shape, dt=F32):
            return ctx.enter_context(nc.sbuf_tensor(name, shape, dt))

        def sem(name):
            return ctx.enter_context(nc.semaphore(name))

        def ts(t):
            return slice(t * P, (t + 1) * P)

        def tiles(ap):
            return ap.rearrange("p (t d) -> p t d", t=NT)

        w1_hi = sb("w1_hi", [P, E, FF], F32R)
        w1_lo = sb("w1_lo", [P, E, FF], F32R)
        w2_hi = sb("w2_hi", [P, E, FC, P], F32R)
        w2_lo = sb("w2_lo", [P, E, FC, P], F32R)
        x_hi = sb("x_hi", [P, N], F32R)
        x_lo = sb("x_lo", [P, N], F32R)
        g = sb("g", [P, 2, N])
        h_hi = sb("h_hi", [P, FC, N], F32R)
        h_lo = sb("h_lo", [P, FC, N], F32R)
        yc = sb("yc", [P, N])
        acc = sb("acc", [P, N])
        acc0 = sb("acc0", [P, N])
        c_bc = sb("c_bc", [P, 2, N])
        x_in = sb("x_in", [P, NT, P])
        x1 = sb("x1", [P, 2 * N])
        ident = sb("ident", [P, P])
        ones = sb("ones", [P, P])
        mask_w = sb("mask_w", [P, P], BF16)
        tri = sb("tri", [P, P], BF16)
        pick_x = sb("pick_x", [2, P])
        pick_y = sb("pick_y", [2, P])
        mhalf_w = sb("mhalf_w", [2, P])
        iota_e = sb("iota_e", [P, E])
        half = sb("half", [P, NT])
        mhalf = sb("mhalf", [P, NT])
        euler = sb("euler", [P, NT * TOP])
        wT = sb("wT", [P, 4, P])
        wtqT = sb("wtqT", [P, 2])
        cols = sb("cols", [P, 70])
        quant_cols = sb("quant_cols", [P, 3])
        wfq_raw = sb("wfq_raw", [P, 2])
        quant_w = sb("quant_w", [67, P])
        btq_bc = sb("btq_bc", [P, 2])
        br2_bc = sb("br2_bc", [P, E])
        wr1 = sb("wr1", [P, P])
        wr2 = sb("wr2", [P, E])
        b2_sb = sb("b2_sb", [E, P])
        st6 = sb("st6", [P, NT, 6])
        mv = sb("mv", [P, NT, 2])
        ve = sb("ve", [P, NT])
        rstd = sb("rstd", [P, NT])
        fst6 = sb("fst6", [P, NT, 6])
        fmv = sb("fmv", [P, NT, 2])
        fve = sb("fve", [P, NT])
        frstd = sb("frstd", [P, NT])
        xn = sb("xn", [P, NT, P])
        xnT = sb("xnT_ady_cT", [P, N])
        ady = xnT
        cT = xnT[0:E, :]
        qT = sb("qT_ctxT", [P, N])
        ctxT = qT
        kT = sb("kT_xfT", [P, N])
        xfT = kT
        v_sb = sb("v_sb", [P, NT, P])
        rows = v_sb
        xbc = sb("xbc_s", [P, N])
        s_sb = tiles(xbc[:, :])
        ybc = sb("ybc_r1T_o", [P, N])
        r1T = ybc
        o_sb = tiles(ybc[:, :])
        cone = sb("cone", [P, N], BF16)
        mask = sb("mask", [P, N], BF16)
        prob = sb("prob_sqT", [P, N * 5 // 2])
        sqT = prob[0:2, 0:N]
        w_raw = prob[:, 0:N].rearrange("p (a d) -> p a d", a=4)
        wtq_row = prob[0:2, N:N + P]
        probT = sb("probT_hit", [P, N * 5 // 2])
        hit = probT[:, 0:NT * TOP * E].rearrange("p (k e) -> p k e", e=E)
        atrt = sb("aT_rT", [P, N])
        aT = atrt[0:2, :]
        rT = atrt[64:67, :]
        qp = sb("qp", [P, NT, 2])
        a = sb("a", [P, NT, 2])
        mean2 = sb("mean2", [P, 2])
        sq = sb("sq", [P, NT, 2])
        nrm = sb("nrm", [P, NT])
        rn = sb("rn", [P, NT])
        r3 = sb("r3", [P, NT, 3])
        mom = sb("mom", [P, 4, NT])
        tot = sb("tot", [P, 4])
        sc = sb("sc", [P, 8])
        nay = sb("nay", [P, NT])
        ax12 = sb("ax12", [P, NT])
        lim = sb("lim", [P, NT])
        nmax = sb("nmax", [P, NT])
        rsum = sb("rsum", [P, NT])
        rinv = sb("rinv", [P, NT])
        lg = sb("lg", [P, NT, E])
        top8 = sb("top8", [P, NT, 8])
        idx8 = sb("idx8", [P, NT, 8], U32)
        idxf = sb("idxf", [P, NT, 8])
        dif = sb("dif", [P, NT * TOP])
        ew = sb("ew", [P, NT * TOP])
        esum = sb("esum", [P, NT])
        einv = sb("einv", [P, NT])
        c_sb = sb("c_sb", [P, NT, E])

        def bank(name):
            return ctx.enter_context(nc.psum_tensor(name, [P, 512], F32))

        A0, A1, A2, A3 = [bank(f"A{i}") for i in range(4)]
        HB = [bank(f"HB{i}") for i in range(2)]
        YB = [bank(f"YB{i}") for i in range(2)]

        SCORES = [A0[:, 0:P], A1[:, 0:2 * P], A0[:, P:4 * P], A2[:, 0:4 * P]]
        PB = [0, P, 3 * P, 6 * P]
        KB = [0, 4 * P, 7 * P, 9 * P]

        def keys(j, lo, hi):
            return probT[:, KB[j] + (lo - j) * P:KB[j] + (hi - j) * P]

        names = """consts_in pool_setup dve_setup pe_setup
            x_loaded pool_order dve_order fin_order
            ln_stats rstd_ready xn_ready xnT_ps xnT_sb qp_ps q_ps k_ps v_ps q_sb k_sb v_ready qp_sb mean_ps a_ready
            mom_ready mom_ps norm_ready rn_ready r3_ready var_ready std_ready aT_ps rT_ps aT_sb rT_sb xbc_ps ybc_ps
            xybc_sb dist_ps ady_ready mask_ready score_ps nmax_ready prob_ready probT_ps probT_act probT_dve ctx_ps
            ctx_sb o_ps s_ready xf_ready x1_ready xfT_ps xfT_sb xhi_ready xlo_ready r1_ps r1_sb logit_ps logit_sb
            dif_ready ew_ready c_ready cT_ps cT_sb cT_stored init_ps init_sb
            w_in0 w_in1 w_hi_done w_lo_done c_in0 c_in1 h_ps g_ready hi_ready split_ready chunk_read y_free y_done
            fin_ps fin_stats fin_rstd fin_out stored dve_gate pool_gate sp_gate""".split()
        S = {n: sem(n) for n in names}

        block = ctx.enter_context(nc.Block())
        BIAS_COL = {"bq": 64, "bk": 65, "bv": 66, "bo": 67, "bfq": 68, "br1": 69}
        NROWS = 70
        NCONST = 4 + 1 + 1 + 1 + 6 + 2 + 2 + 1

        def col(name):
            return cols[:, BIAS_COL[name]:BIAS_COL[name] + 1]

        def x1_of(b):
            return tiles(x1[:, bass.ds((b % 2) * N, N)])

        def raw_of(e):
            return (c_bc, g)[e % 2][:, :, :].rearrange("p a n -> p (a n)")

        def run(ffn, att, fin, fb, stages, final, after=None):
            for k in range(SLOTS):
                if ffn:
                    ffn(fb, k)
                if fin and k in final:
                    final[k](fb - 1)
                if att and k in stages:
                    stages[k](fb + 1)
                if after:
                    after(k)

        def iterations(eng, ffn, stages, final, prologue=None):
            run(None, True, False, -1, stages, final, prologue)
            run(ffn, True, False, 0, stages, final)
            with eng.Fori(1, B - 1) as b:
                run(ffn, True, True, b, stages, final)
            run(ffn, False, True, B - 1, stages, final)

        @block.sync
        def _(sp):
            n = 0

            def const(dst, src):
                nonlocal n
                sp.dma_start(dst, src).then_inc(S["consts_in"], 16)
                n += 1

            def load_x(b):
                src = x_d[b] if isinstance(b, int) else x_d[bass.ds(b, 1)].rearrange("o n d -> (o n) d")
                sp.dma_start(x_in[:, :, :], src.rearrange("(t p) d -> p t d", p=P)).then_inc(S["x_loaded"], 16)

            def load_w(e):
                raw = raw_of(e)
                if e >= 2:
                    sp.wait_ge(S["w_lo_done"], e - 1)
                sp.dma_start(raw[:, 0:FF], W1[e]).then_inc(S[f"w_in{e % 2}"], 16)
                sp.dma_start(raw[:, FF:2 * FF].rearrange("p (c h) -> p c h", h=P),
                             W2[e].rearrange("(c p) h -> p c h", p=P)).then_inc(S[f"w_in{e % 2}"], 16)

            load_x(0)
            for i, w in enumerate((Wq, Wk, Wv, Wo)):
                const(w_raw[:, i, :], w)
            const(wtq_row, Wtq)
            const(wfq_raw[:, :], Wfq)
            const(rows[0:E * FC, 0, :], b1.rearrange("e (c p) -> (e c) p", p=P))
            for name, v in (("bq", bq), ("bk", bk), ("bv", bv), ("bo", bo), ("bfq", bfq), ("br1", br1)):
                const(rows[BIAS_COL[name]:BIAS_COL[name] + 1, 0, :], v.rearrange("(o d) -> o d", o=1))
            const(btq_bc[:, :], btq.partition_broadcast(P))
            const(br2_bc[:, :], br2.partition_broadcast(P))
            const(wr1[:, :], Wr1)
            const(wr2[:, :], Wr2)
            const(b2_sb[:, :], b2)
            assert n == NCONST
            for e in range(WEIGHTS_BEFORE_SOFTMAX):
                load_w(e)

            def store_c(b):
                sp.wait_ge(S["cT_sb"], b + 1)
                sp.dma_start(cT_d[:, bass.ds(b * N, N)], cT).then_inc(S["cT_stored"], 16)

            def load_c(b, e):
                if not (isinstance(b, int) and b == 0 and e < 2):
                    sp.wait_ge(S["y_done"], E * b + e - 1)
                if e == 0:
                    sp.sem_inc(S["sp_gate"], 1)
                    sp.wait_ge(S["cT_stored"], 16 * b + 16)
                sp.dma_start(c_bc[:, e % 2, :], cT_d[e:e + 1, bass.ds(b * N, N)].broadcast_to([P, N])
                             ).then_inc(S[f"c_in{e % 2}"], 16)

            def iteration(b, att, fin):
                for e in range(2, E):
                    load_c(b, e)
                    if e == 3 and fin:
                        sp.wait_ge(S["fin_out"], b)
                        sp.dma_start(out_d[bass.ds(b - 1, 1)].rearrange("o (t p) d -> p (o t) d", p=P), o_sb
                                     ).then_inc(S["stored"], 16)
                    if e == 12 and att == 2:
                        sp.wait_ge(S["x1_ready"], b + 2)
                        load_x(b + 2)
                if att:
                    store_c(b + 1)
                    load_c(b + 1, 0)
                    load_c(b + 1, 1)

            sp.wait_ge(S["x1_ready"], 1)
            load_x(1)
            store_c(0)
            sp.wait_ge(S["w_lo_done"], E)
            load_c(0, 0)
            load_c(0, 1)
            iteration(0, 2, False)
            with sp.Fori(1, B - 2) as b:
                iteration(b, 2, True)
            iteration(B - 2, 1, True)
            iteration(B - 1, 0, True)
            sp.wait_ge(S["fin_out"], B)
            sp.dma_start(out_d[B - 1].rearrange("(t p) d -> p t d", p=P), o_sb).then_inc(S["stored"], 16)
            sp.wait_ge(S["stored"], 16 * B)

        @block.gpsimd
        def _(pool):
            G = nc.gpsimd
            order = 0

            def setup(ins):
                nonlocal order
                order += 1
                ins.then_inc(S["pool_setup"], 1)
                pool.wait_ge(S["pool_setup"], order)

            setup(G.memset(ident[:, :], 0.0))
            setup(G.affine_select(out=ident[:, :], in_=ident[:, :], compare_op=ALU.not_equal, fill=1.0, base=0,
                                  pattern=[[-1, P]], channel_multiplier=1))
            for tile, value in ((mask_w, 0.0), (tri, 0.0), (ones, 1.0), (half, 0.5), (mhalf, -0.5), (mhalf_w, -0.5),
                                (euler, EULER), (pick_x, 0.0), (pick_y, 1.0)):
                setup(G.memset(tile[:, :], value))
            setup(G.memset(r3[:, :, :], 1.0))
            setup(G.memset(pick_x[0:1, :], 1.0))
            setup(G.memset(pick_y[0:1, :], 0.0))
            setup(G.affine_select(out=mask_w[:, :], in_=mask_w[:, :], compare_op=ALU.not_equal, fill=MASKED, base=0,
                                  pattern=[[-1, P]], channel_multiplier=1))
            setup(G.affine_select(out=tri[:, :], in_=tri[:, :], compare_op=ALU.is_ge, fill=1.0, base=0,
                                  pattern=[[-1, P]], channel_multiplier=1))
            setup(G.iota(iota_e[:, :], pattern=[[1, E]], base=0, channel_multiplier=0,
                         allow_small_or_imprecise_dtypes=True))
            assert order == POOL_SETUP

            def own_wait():
                pool.sem_inc(S["pool_gate"], 1)

            def inverse_std(src, tmp, dst, order_value, dst_sem):
                own_wait()
                G.tensor_scalar(tmp[:, :], src[:, :, 1], EPS, None, ALU.add).then_inc(S["pool_order"], 1)
                pool.wait_ge(S["pool_order"], order_value)
                G.tensor_tensor(dst[:, :], tmp[:, :], mhalf[:, :], ALU.pow).then_inc(S[dst_sem], 1)

            def iteration(b, att, fin):
                done = 3 * b if att else 3 * B
                done_fin = b - 2 if fin else 0
                if att:
                    pool.wait_ge(S["ln_stats"], 3 * b + 1)
                    inverse_std(mv, ve, rstd, done + done_fin + 1, "rstd_ready")
                    done = done + 1
                if fin:
                    pool.wait_ge(S["fin_stats"], b - 1)
                    inverse_std(fmv, fve, frstd, done + done_fin + 1, "fin_rstd")
                    done_fin = done_fin + 1
                if att:
                    pool.wait_ge(S["norm_ready"], b + 1)
                    G.tensor_tensor(rn[:, :], nrm[:, :], mhalf[:, :], ALU.pow).then_inc(S["rn_ready"], 1)
                    pool.wait_ge(S["var_ready"], b + 1)
                    G.tensor_tensor(sc[:, 6:7], sc[:, 5:6], half[:, 0:1], ALU.pow).then_inc(S["std_ready"], 1)
                    for i in (2, 3):
                        pool.wait_ge(S["ln_stats"], 3 * b + i)
                        inverse_std(mv, ve, rstd, done + done_fin + i - 1, "rstd_ready")
                    pool.wait_ge(S["dif_ready"], b + 1)
                    G.tensor_tensor(ew[:, :], euler[:, :], dif[:, :], ALU.pow).then_inc(S["ew_ready"], 1)

            iteration(0, True, False)
            iteration(1, True, False)
            with pool.Fori(2, B) as b:
                iteration(b, True, True)
            iteration(B, False, True)
            iteration(B + 1, False, True)

        @block.vector
        def _(dve):
            V = nc.vector
            n = 0

            def setup(ins):
                nonlocal n
                n += 1
                ins.then_inc(S["dve_setup"], 1)

            dve.wait_ge(S["pe_setup"], 1)
            setup(V.tensor_copy(wT[:, :, :].rearrange("p a d -> p (a d)"), A0[:, :]))
            setup(V.tensor_copy(wtqT[:, :], A1[:, 0:2]))
            setup(V.tensor_copy(cols[:, 0:NROWS], A1[:, P:P + NROWS]))
            dve.wait_ge(S["dve_setup"], 3)
            setup(V.tensor_scalar(quant_cols[:, 0:2], wfq_raw[:, :], QUANTUM, None, ALU.mult))
            dve.wait_ge(S["pe_setup"], 2)
            setup(V.tensor_tensor(quant_cols[:, 2:3], A2[:, 0:1], col("bo"), ALU.add))
            dve.wait_ge(S["dve_setup"], 5)
            setup(V.scalar_tensor_tensor(quant_cols[:, 2:3], col("bfq"), QUANTUM, quant_cols[:, 2:3], ALU.mult, ALU.add))
            dve.wait_ge(S["pe_setup"], 3)
            setup(V.tensor_copy(quant_w[64:67, :], A3[0:3, 0:P]))
            assert n == DVE_SETUP

            def own_wait():
                dve.sem_inc(S["dve_gate"], 1)

            def stats(st, src):
                for t in range(NT):
                    last = V.bn_stats(st[:, t, :], src[:, t, :])
                return last

            def aggregate(m, st):
                own_wait()
                for t in range(NT):
                    last = V.bn_aggr(m[:, t, :], st[:, t, :])
                return last

            def normalise(dst, src, m, r):
                for t in range(NT):
                    last = V.tensor_scalar(dst[:, t, :], src[:, t, :], m[:, t, 0:1], r[:, t:t + 1],
                                           ALU.subtract, ALU.mult)
                return last

            linked = {"n": 0}

            def link(b, ins):
                linked["n"] += 1
                ins.then_inc(S["dve_order"], 1)
                dve.wait_ge(S["dve_order"], b * DVE_ORDER + linked["n"])

            def norm_in(b):
                linked["n"] = 0
                dve.wait_ge(S["x_loaded"], 16 * b + 16)
                own_wait()
                link(b, stats(st6, x_in))
                aggregate(mv, st6).then_inc(S["ln_stats"], 1)

            def normed(b):
                dve.wait_ge(S["rstd_ready"], 3 * b + 1)
                normalise(xn, x_in, mv, rstd).then_inc(S["xn_ready"], 1)

            def quantum(b):
                dve.wait_ge(S["qp_ps"], b + 1)
                V.tensor_tensor(qp[:, :, :], A0[:, 0:2 * NT].rearrange("p (t c) -> p t c", c=2),
                                btq_bc[:, :].unsqueeze(1).broadcast_to([P, NT, 2]), ALU.add).then_inc(S["qp_sb"], 1)
                dve.wait_ge(S["qp_sb"], b + 1)
                link(b, V.tensor_tensor(sq[:, :, :], qp[:, :, :], qp[:, :, :], ALU.mult))
                link(b, V.tensor_tensor(nrm[:, :], sq[:, :, 0], sq[:, :, 1], ALU.add))
                V.tensor_scalar(nrm[:, :], nrm[:, :], TINY_NORM ** 2, None, ALU.max).then_inc(S["norm_ready"], 1)

            def centre(b):
                dve.wait_ge(S["mean_ps"], b + 1)
                link(b, V.tensor_reduce(mean2[:, :], A0[:, 2 * NT:4 * NT].rearrange("p (t c) -> p c t", c=2),
                                        AX_X, ALU.add))
                V.scalar_tensor_tensor(a[:, :, :], mean2[:, :].unsqueeze(1).broadcast_to([P, NT, 2]), -1.0 / N,
                                       qp[:, :, :], ALU.mult, ALU.add).then_inc(S["a_ready"], 1)
                dve.wait_ge(S["k_ps"], b + 1)
                V.tensor_scalar(kT[:, :], A2[:, :], col("bk"), SCALE, ALU.add, ALU.mult).then_inc(S["k_sb"], 1)

            def moments(b):
                dve.wait_ge(S["a_ready"], b + 1)
                V.tensor_tensor(mom[:, 0, :], a[:, :, 0], a[:, :, 0], ALU.mult)
                V.tensor_tensor(mom[:, 1, :], a[:, :, 1], a[:, :, 1], ALU.mult)
                link(b, V.tensor_tensor(mom[:, 2, :], a[:, :, 0], a[:, :, 1], ALU.mult))
                dve.wait_ge(S["rn_ready"], b + 1)
                link(b, V.tensor_tensor(nrm[:, :], mom[:, 0, :], mom[:, 1, :], ALU.add))
                V.tensor_tensor(mom[:, 3, :], nrm[:, :], nrm[:, :], ALU.mult).then_inc(S["mom_ready"], 1)
                V.tensor_tensor(r3[:, :, 0:2], qp[:, :, :], rn[:, :].unsqueeze(2).broadcast_to([P, NT, 2]),
                                ALU.mult).then_inc(S["r3_ready"], 1)
                V.tensor_scalar(nay[:, :], a[:, :, 1], -1.0, None, ALU.mult)
                V.tensor_scalar(ax12[:, :], a[:, :, 0], PI_CONE, None, ALU.mult)

            def variance(b):
                dve.wait_ge(S["mom_ps"], b + 1)
                link(b, V.tensor_reduce(tot[:, :], A0[:, 4 * NT:8 * NT].rearrange("p (q t) -> p q t", t=NT),
                                        AX_X, ALU.add))
                sxx, syy, sxy, snn = (tot[:, i:i + 1] for i in range(4))
                link(b, V.tensor_tensor(sc[:, 0:1], sxx, syy, ALU.add))
                link(b, V.scalar_tensor_tensor(sc[:, 1:2], sc[:, 0:1], -0.5, sc[:, 0:1], ALU.mult, ALU.mult))
                link(b, V.scalar_tensor_tensor(sc[:, 1:2], snn, N / 2.0, sc[:, 1:2], ALU.mult, ALU.add))
                link(b, V.scalar_tensor_tensor(sc[:, 2:3], sxx, sxx, sc[:, 1:2], ALU.mult, ALU.add))
                link(b, V.scalar_tensor_tensor(sc[:, 3:4], syy, syy, sc[:, 2:3], ALU.mult, ALU.add))
                link(b, V.tensor_tensor(sc[:, 4:5], sxy, sxy, ALU.mult))
                link(b, V.scalar_tensor_tensor(sc[:, 4:5], sc[:, 4:5], 2.0, sc[:, 3:4], ALU.mult, ALU.add))
                V.tensor_scalar(sc[:, 5:6], sc[:, 4:5], 4.0 / (PAIRS - 1.0), 0.0, ALU.mult, ALU.max
                                ).then_inc(S["var_ready"], 1)

            def threshold(b):
                dve.wait_ge(S["std_ready"], b + 1)
                link(b, V.tensor_scalar(sc[:, 7:8], sc[:, 6:7], THRESHOLD_FACTOR, None, ALU.mult))
                link(b, V.scalar_tensor_tensor(sc[:, 7:8], sc[:, 0:1], 2.0 / N, sc[:, 7:8], ALU.mult, ALU.add))
                link(b, V.tensor_scalar(lim[:, :], nrm[:, :], sc[:, 7:8], 0.5, ALU.subtract, ALU.mult))

            def pair_mask(t):
                def stage(b):
                    w = P * (t + 1)
                    dve.wait_ge(S["ady_ready"], NT * b + t + 1)
                    link(b, V.scalar_tensor_tensor(cone[:, 0:w], xbc[:, 0:w], ax12[:, t:t + 1], ady[:, 0:w],
                                                   ALU.subtract, ALU.is_gt))
                    if t >= 1:
                        dve.wait_ge(S["score_ps"], NT * b + t)
                    dve.wait_ge(S["dist_ps"], NT * b + t + 1)
                    V.scalar_tensor_tensor(mask[:, 0:w], A3[:, 0:w], lim[:, t:t + 1], cone[:, 0:w],
                                           ALU.is_lt, ALU.max).then_inc(S["mask_ready"], 1)
                return stage

            def row_max(t):
                def stage(b):
                    dve.wait_ge(S["score_ps"], NT * b + t + 1)
                    V.tensor_reduce(nmax[:, t:t + 1], SCORES[t], AX_X, ALU.max, negate=True).then_inc(S["nmax_ready"], 1)
                return stage

            def turn_prob(b):
                dve.wait_ge(S["probT_ps"], 3 * b + 2)
                for j in range(3):
                    last = V.tensor_copy(keys(j, 2, 3), A1[:, ts(j)])
                last.then_inc(S["probT_dve"], 1)

            def residual(b):
                dve.wait_ge(S["prob_ready"], b + 1)
                link(b, V.reciprocal(rinv[:, :], rsum[:, :]))
                dve.wait_ge(S["o_ps"], b + 1)
                for t in range(NT):
                    last = V.scalar_tensor_tensor(s_sb[:, t, :], A0[:, ts(t)], rinv[:, t:t + 1], xn[:, t, :],
                                                  ALU.mult, ALU.add)
                link(b, last)
                V.tensor_tensor(s_sb, tiles(A1[:, :]), s_sb, ALU.add).then_inc(S["s_ready"], 1)

            def norm_attention(b):
                dve.wait_ge(S["s_ready"], b + 1)
                own_wait()
                link(b, stats(st6, s_sb))
                aggregate(mv, st6).then_inc(S["ln_stats"], 1)

            def add_attention(b):
                dve.wait_ge(S["rstd_ready"], 3 * b + 2)
                link(b, normalise(s_sb, s_sb, mv, rstd))
                V.tensor_tensor(x1_of(b), x_in[:, :, :], s_sb, ALU.add).then_inc(S["x1_ready"], 1)

            def norm_ffn(b):
                dve.wait_ge(S["x1_ready"], b + 1)
                own_wait()
                link(b, stats(st6, x1_of(b)))
                aggregate(mv, st6).then_inc(S["ln_stats"], 1)

            def ffn_input(b):
                dve.wait_ge(S["rstd_ready"], 3 * b + 3)
                normalise(s_sb, x1_of(b), mv, rstd).then_inc(S["xf_ready"], 1)

            def choose(b):
                dve.wait_ge(S["logit_ps"], b + 1)
                V.tensor_tensor(lg[:, :, :], A0[:, 0:NT * E].rearrange("p (t e) -> p t e", e=E),
                                br2_bc[:, :].unsqueeze(1).broadcast_to([P, NT, E]), ALU.add).then_inc(S["logit_sb"], 1)
                dve.wait_ge(S["logit_sb"], b + 1)
                own_wait()
                for t in range(NT):
                    last = V.max(top8[:, t, :], lg[:, t, :])
                link(b, last)
                V.tensor_tensor(dif[:, :].rearrange("p (t k) -> p t k", k=TOP), top8[:, :, 0:TOP],
                                top8[:, :, 0:1].broadcast_to([P, NT, TOP]), ALU.subtract).then_inc(S["dif_ready"], 1)

            def chosen(b):
                for t in range(NT):
                    last = V.max_index(idx8[:, t, :], top8[:, t, :], lg[:, t, :])
                link(b, last)
                link(b, V.tensor_copy(idxf[:, :, :], idx8[:, :, :]))
                h4 = hit.rearrange("p (t k) e -> p t k e", k=TOP)
                for t in range(NT):
                    last = V.tensor_tensor(h4[:, t], idxf[:, t, 0:TOP].unsqueeze(2).broadcast_to([P, TOP, E]),
                                           iota_e[:, :].unsqueeze(1).broadcast_to([P, TOP, E]), ALU.is_equal)
                link(b, last)

            def routing(b):
                dve.wait_ge(S["ew_ready"], b + 1)
                ew4 = ew[:, :].rearrange("p (t k) -> p t k", k=TOP)
                link(b, V.tensor_reduce(esum[:, :], ew4, AX_X, ALU.add))
                link(b, V.reciprocal(einv[:, :], esum[:, :]))
                link(b, V.tensor_tensor(ew4, ew4, einv[:, :].unsqueeze(2).broadcast_to([P, NT, TOP]), ALU.mult))
                link(b, V.tensor_tensor(hit, hit, ew[:, :].unsqueeze(2).broadcast_to([P, NT * TOP, E]), ALU.mult))
                V.tensor_reduce(c_sb[:, :, :], hit.rearrange("p (t k) e -> p t e k", k=TOP), AX_X, ALU.add
                                ).then_inc(S["c_ready"], 1)

            def turn_routing(b):
                dve.wait_ge(S["cT_ps"], b + 1)
                V.tensor_copy(cT, A1[0:E, :]).then_inc(S["cT_sb"], 1)

            def start_acc(b):
                dve.wait_ge(S["init_ps"], b + 1)
                V.tensor_copy(acc0[:, :], A2[:, :]).then_inc(S["init_sb"], 1)
                assert linked["n"] == DVE_ORDER, linked

            def split_input(b):
                if not (isinstance(b, int) and b == 0):
                    dve.wait_ge(S["h_ps"], SLOTS * b)
                V.tensor_copy(x_hi[:, :], xfT[:, :]).then_inc(S["xhi_ready"], 1)
                dve.wait_ge(S["xhi_ready"], b + 1)
                V.tensor_tensor(x_lo[:, :], xfT[:, :], x_hi[:, :].bitcast(F32), ALU.subtract
                                ).then_inc(S["xlo_ready"], 1)

            stages = {0: norm_in, 2: normed, 6: quantum, 8: centre, 10: moments, 12: variance, 14: threshold,
                      16: pair_mask(0), 18: row_max(0), 19: pair_mask(1), 21: row_max(1), 22: pair_mask(2),
                      24: row_max(2), 25: pair_mask(3), 27: row_max(3), 32: turn_prob, 37: residual,
                      38: norm_attention, 40: add_attention, 41: norm_ffn, 43: ffn_input, 49: choose, 50: chosen,
                      52: routing, 54: turn_routing, 56: start_acc, 62: split_input}

            def last_stats(b):
                dve.wait_ge(S["fin_ps"], b + 1)
                own_wait()
                stats(fst6, tiles(A3[:, :])).then_inc(S["fin_order"], 1)
                dve.wait_ge(S["fin_order"], 2 * b + 1)
                aggregate(fmv, fst6).then_inc(S["fin_stats"], 1)

            def last_norm(b):
                dve.wait_ge(S["fin_rstd"], b + 1)
                normalise(o_sb, tiles(A3[:, :]), fmv, frstd).then_inc(S["fin_order"], 1)
                dve.wait_ge(S["fin_order"], 2 * b + 2)
                V.tensor_tensor(o_sb, o_sb, x1_of(b), ALU.add).then_inc(S["fin_out"], 1)

            final = {5: last_stats, 7: last_norm}

            def accumulate(u, b, e):
                dve.wait_ge(S["chunk_read"], FC * (u + 1))
                dve.wait_ge(S[f"c_in{e % 2}"], 8 * E * b + 16 * (e // 2 + 1))
                V.tensor_tensor(yc[:, :], YB[e % 2][:, :], c_bc[:, e % 2, :], ALU.mult).then_inc(S["y_free"], 1)
                dve.wait_ge(S["y_free"], 2 + u + 1)
                V.tensor_tensor(acc[:, :], (acc if e else acc0)[:, :], yc[:, :], ALU.add).then_inc(S["y_done"], 1)

            def ffn(b, k):
                e, c = divmod(k, FC)
                kk = SLOTS * b + k
                first = isinstance(b, int) and kk < FC
                dve.wait_ge(S["g_ready"], kk + 1)
                if not first:
                    dve.wait_ge(S["chunk_read"], kk - FC + 1)
                if c not in SCALAR_HALVES:
                    V.tensor_copy(h_hi[:, c, :], g[:, c % 2, :]).then_inc(S["hi_ready"], 1)
                    dve.wait_ge(S["hi_ready"], DVE_HALVES * (E * b + e)
                                + [i for i in range(FC) if i not in SCALAR_HALVES].index(c) + 1)
                V.tensor_tensor(h_lo[:, c, :], g[:, c % 2, :], h_hi[:, c, :].bitcast(F32), ALU.subtract
                                ).then_inc(S["split_ready"], 1)
                if c == FC - 1 and not first:
                    if e:
                        accumulate(E * b + e - 1, b, e - 1)
                    elif not (isinstance(b, int) and b == 0):
                        accumulate(E * b - 1, b - 1, E - 1)

            DVE_HALVES = FC - len(SCALAR_HALVES)

            def prologue(k):
                for e in PROLOGUE.get(k, ()):
                    raw = raw_of(e)
                    dve.wait_ge(S["w_hi_done"], e + 1)
                    V.tensor_tensor(w1_lo[:, e, :], raw[:, 0:FF], w1_hi[:, e, :].bitcast(F32), ALU.subtract)
                    V.tensor_tensor(w2_lo[:, e, :, :].rearrange("p c h -> p (c h)"), raw[:, FF:2 * FF],
                                    w2_hi[:, e, :, :].rearrange("p c h -> p (c h)").bitcast(F32), ALU.subtract
                                    ).then_inc(S["w_lo_done"], 1)

            dve.sem_inc(S["y_free"], 2)
            iterations(dve, ffn, stages, final, prologue)
            dve.wait_ge(S["y_done"], E * B - 1)
            accumulate(E * B - 1, B - 1, E - 1)
            last_stats(B - 1)
            last_norm(B - 1)

        @block.scalar
        def _(act):
            A = nc.scalar
            act.wait_ge(S["dve_setup"], DVE_SETUP)

            def turned_xn(b):
                act.wait_ge(S["xnT_ps"], b + 1)
                if not (isinstance(b, int) and b == 0):
                    act.wait_ge(S["cT_stored"], 16 * b)
                A.copy(xnT[:, :], A0[:, :]).then_inc(S["xnT_sb"], 1)

            def query(b):
                act.wait_ge(S["q_ps"], b + 1)
                A.activation(qT[:, :], A1[:, :], ACT.Identity, bias=col("bq")).then_inc(S["q_sb"], 1)

            def value(b):
                act.wait_ge(S["v_ps"], b + 1)
                A.copy(v_sb[:, :, :].rearrange("p t d -> p (t d)"), A3[:, :]).then_inc(S["v_ready"], 1)

            def coordinate_rows(b):
                act.wait_ge(S["aT_ps"], b + 1)
                A.copy(aT, A1[0:2, :])
                A.activation(sqT, A1[0:2, :], ACT.Square).then_inc(S["aT_sb"], 1)
                act.wait_ge(S["rT_ps"], b + 1)
                A.copy(rT, A2[0:3, :]).then_inc(S["rT_sb"], 1)

            def coordinate_tiles(b):
                act.wait_ge(S["xbc_ps"], b + 1)
                A.mul(xbc[:, :], A1[:, :], PI_CONE)
                act.wait_ge(S["ybc_ps"], b + 1)
                if not (isinstance(b, int) and b < 2):
                    act.wait_ge(S["stored"], 16 * (b - 1))
                A.copy(ybc[:, :], A2[:, :]).then_inc(S["xybc_sb"], 1)

            def abs_dy(t):
                def stage(b):
                    w = P * (t + 1)
                    if t == 0:
                        act.wait_ge(S["xybc_sb"], b + 1)
                        act.wait_ge(S["r3_ready"], b + 1)
                        act.wait_ge(S["var_ready"], b + 1)
                    else:
                        act.wait_ge(S["mask_ready"], NT * b + t)
                    A.activation(ady[:, 0:w], ybc[:, 0:w], ACT.Abs, bias=nay[:, t:t + 1]).then_inc(S["ady_ready"], 1)
                return stage

            def softmax(b):
                act.wait_ge(S["nmax_ready"], NT * b + NT)
                for t in range(NT):
                    m = A.activation(prob[:, PB[t]:PB[t] + P * (t + 1)], SCORES[t], ACT.Exp, bias=nmax[:, t:t + 1],
                                     accum_out=rsum[:, t:t + 1])
                m.then_inc(S["prob_ready"], 1)

            def turn_prob3(b):
                act.wait_ge(S["probT_ps"], 3 * b + 1)
                for j in range(NT):
                    m = A.copy(keys(j, 3, 4), A0[:, ts(j)])
                m.then_inc(S["probT_act"], 1)

            def turn_prob01(b):
                act.wait_ge(S["probT_ps"], 3 * b + 3)
                A.copy(keys(0, 0, 2), A2[:, 0:2 * P])
                A.copy(keys(1, 1, 2), A2[:, 2 * P:3 * P]).then_inc(S["probT_act"], 1)

            def context(b):
                act.wait_ge(S["ctx_ps"], b + 1)
                A.copy(ctxT[:, :], A3[:, :]).then_inc(S["ctx_sb"], 1)

            def turned_xf(b):
                act.wait_ge(S["xfT_ps"], b + 1)
                A.copy(xfT[:, :], A2[:, :]).then_inc(S["xfT_sb"], 1)

            def router_hidden(b):
                act.wait_ge(S["r1_ps"], b + 1)
                A.activation(r1T[:, :], A3[:, :], ACT.Relu, bias=col("br1")).then_inc(S["r1_sb"], 1)

            stages = {4: turned_xn, 6: query, 10: value, 12: coordinate_rows, 14: coordinate_tiles,
                      16: abs_dy(0), 19: abs_dy(1), 22: abs_dy(2), 25: abs_dy(3), 29: softmax,
                      31: turn_prob3, 33: turn_prob01, 35: context, 45: turned_xf, 47: router_hidden}

            def ffn(b, k):
                e, c = divmod(k, FC)
                kk = SLOTS * b + k
                first = isinstance(b, int) and kk < FC
                act.wait_ge(S["h_ps"], kk + 1)
                if not (isinstance(b, int) and kk < 2):
                    act.wait_ge(S["split_ready"], kk - 1)
                bias = cols[:, k:k + 1]
                if c in SCALAR_HALVES:
                    if not first:
                        act.wait_ge(S["chunk_read"], kk - FC + 1)
                    A.activation(h_hi[:, c, :], HB[c % 2][:, :], ACT.Gelu, bias=bias)
                A.activation(g[:, c % 2, :], HB[c % 2][:, :], ACT.Gelu, bias=bias).then_inc(S["g_ready"], 1)

            def prologue(k):
                for e in PROLOGUE.get(k, ()):
                    raw = raw_of(e)
                    act.wait_ge(S[f"w_in{e % 2}"], 32 * (e // 2 + 1))
                    A.copy(w1_hi[:, e, :], raw[:, 0:FF])
                    A.copy(w2_hi[:, e, :, :].rearrange("p c h -> p (c h)"), raw[:, FF:2 * FF]
                           ).then_inc(S["w_hi_done"], 1)

            iterations(act, ffn, stages, {}, prologue)

        @block.tensor
        def _(pe):
            T = nc.tensor
            pe.wait_ge(S["consts_in"], 16 * NCONST)
            pe.wait_ge(S["pool_setup"], POOL_SETUP)
            for i in range(4):
                T.transpose(A0[:, ts(i)], w_raw[:, i, :], ident[:, :])
            T.transpose(A1[:, 0:2], wtq_row, ident[0:2, 0:2])
            T.transpose(A1[:, P:P + NROWS], rows[0:NROWS, 0, :], ident[0:NROWS, 0:NROWS]).then_inc(S["pe_setup"], 1)
            pe.wait_ge(S["dve_setup"], 3)
            T.matmul(A2[:, 0:1], wT[:, 3, :], col("bv"), start=True, stop=True).then_inc(S["pe_setup"], 1)
            pe.wait_ge(S["dve_setup"], 6)
            T.transpose(A3[0:3, 0:P], quant_cols[:, :], ident[:, :]).then_inc(S["pe_setup"], 1)
            pe.wait_ge(S["dve_setup"], DVE_SETUP)

            def turn_xn(b):
                pe.wait_ge(S["xn_ready"], b + 1)
                if not (isinstance(b, int) and b == 0):
                    pe.wait_ge(S["logit_sb"], b)
                for t in range(NT):
                    last = T.transpose(A0[:, ts(t)], xn[:, t, :], ident[:, :])
                last.then_inc(S["xnT_ps"], 1)

            def quantum_query(b):
                pe.wait_ge(S["xnT_sb"], b + 1)
                for t in range(NT):
                    last = T.matmul(A0[:, 2 * t:2 * t + 2], xnT[:, ts(t)], wtqT[:, :], start=True, stop=True)
                last.then_inc(S["qp_ps"], 1)
                if not (isinstance(b, int) and b == 0):
                    pe.wait_ge(S["cT_sb"], b)
                T.matmul(A1[:, :], wT[:, 0, :], xnT[:, :], start=True, stop=True).then_inc(S["q_ps"], 1)

            def mean_key(b):
                pe.wait_ge(S["qp_sb"], b + 1)
                T.matmul(A0[:, 2 * NT:4 * NT], ones[:, :], qp[:, :, :].rearrange("p t c -> p (t c)"),
                         start=True, stop=True).then_inc(S["mean_ps"], 1)
                if not (isinstance(b, int) and b == 0):
                    pe.wait_ge(S["init_sb"], b)
                T.matmul(A2[:, :], wT[:, 1, :], xnT[:, :], start=True, stop=True).then_inc(S["k_ps"], 1)

            def values(b):
                if not (isinstance(b, int) and b < 2):
                    pe.wait_ge(S["fin_out"], b - 1)
                for t in range(NT):
                    last = T.matmul(A3[:, ts(t)], xnT[:, ts(t)], wT[:, 2, :], start=True, stop=True)
                last.then_inc(S["v_ps"], 1)

            def coordinates(b):
                pe.wait_ge(S["a_ready"], b + 1)
                pe.wait_ge(S["q_sb"], b + 1)
                for t in range(NT):
                    last = T.transpose(A1[0:2, ts(t)], a[:, t, :], ident[:, :])
                last.then_inc(S["aT_ps"], 1)
                pe.wait_ge(S["mom_ready"], b + 1)
                T.matmul(A0[:, 4 * NT:8 * NT], ones[:, :], mom[:, :, :].rearrange("p q t -> p (q t)"),
                         start=True, stop=True).then_inc(S["mom_ps"], 1)
                pe.wait_ge(S["r3_ready"], b + 1)
                pe.wait_ge(S["k_sb"], b + 1)
                for t in range(NT):
                    last = T.transpose(A2[0:3, ts(t)], r3[:, t, :], ident[:, :])
                last.then_inc(S["rT_ps"], 1)

            def spread(b):
                pe.wait_ge(S["aT_sb"], b + 1)
                T.matmul(A1[:, :], pick_x[:, :], aT, start=True, stop=True).then_inc(S["xbc_ps"], 1)
                pe.wait_ge(S["rT_sb"], b + 1)
                T.matmul(A2[:, :], pick_y[:, :], aT, start=True, stop=True).then_inc(S["ybc_ps"], 1)

            def distance(t):
                def stage(b):
                    w = P * (t + 1)
                    if t == 0:
                        pe.wait_ge(S["v_ready"], b + 1)
                    else:
                        pe.wait_ge(S["mask_ready"], NT * b + t)
                    T.matmul(A3[:, 0:w], aT[:, ts(t)], aT[:, 0:w], start=True, stop=False)
                    T.matmul(A3[:, 0:w], mhalf_w[:, :], sqT[:, 0:w], start=False, stop=True).then_inc(S["dist_ps"], 1)
                return stage

            def scores(t):
                def stage(b):
                    w = P * (t + 1)
                    s = SCORES[t]
                    if t == 0:
                        pe.wait_ge(S["var_ready"], b + 1)
                        pe.wait_ge(S["xybc_sb"], b + 1)
                    if t == 2:
                        pe.wait_ge(S["nmax_ready"], NT * b + 1)
                    T.matmul(s, qT[:, ts(t)], kT[:, 0:w], start=True, stop=False)
                    T.matmul(s[:, ts(t)], mask_w[:, :], tri[:, :], start=False, stop=False)
                    pe.wait_ge(S["mask_ready"], NT * b + t + 1)
                    T.matmul(s, mask_w[:, :], mask[:, 0:w], start=False, stop=True).then_inc(S["score_ps"], 1)
                return stage

            def transpose_prob(b):
                pe.wait_ge(S["prob_ready"], b + 1)
                for t, dst in ((3, [A0[:, ts(j)] for j in range(4)]), (2, [A1[:, ts(j)] for j in range(3)])):
                    for j in range(t + 1):
                        last = T.transpose(dst[j], prob[:, PB[t] + j * P:PB[t] + (j + 1) * P], ident[:, :])
                    last.then_inc(S["probT_ps"], 1)
                T.transpose(A2[:, ts(0)], prob[:, PB[0]:PB[0] + P], ident[:, :])
                T.transpose(A2[:, ts(1)], prob[:, PB[1]:PB[1] + P], ident[:, :])
                T.transpose(A2[:, ts(2)], prob[:, PB[1] + P:PB[1] + 2 * P], ident[:, :]).then_inc(S["probT_ps"], 1)

            def weigh_values(b):
                pe.wait_ge(S["probT_act"], 2 * b + 2)
                pe.wait_ge(S["probT_dve"], b + 1)
                for j in range(NT):
                    last = T.matmul(A3[:, j * P:N], v_sb[:, j, :], keys(j, j, NT), start=(j == 0), stop=(j == NT - 1))
                last.then_inc(S["ctx_ps"], 1)

            def output(b):
                for t in range(NT):
                    T.matmul(A1[:, ts(t)], rT[:, ts(t)], quant_w[64:67, :], start=True, stop=True)
                pe.wait_ge(S["ctx_sb"], b + 1)
                for t in range(NT):
                    last = T.matmul(A0[:, ts(t)], ctxT[:, ts(t)], wT[:, 3, :], start=True, stop=True)
                last.then_inc(S["o_ps"], 1)

            def turn_xf(b):
                pe.wait_ge(S["xf_ready"], b + 1)
                for t in range(NT):
                    last = T.transpose(A2[:, ts(t)], s_sb[:, t, :], ident[:, :])
                last.then_inc(S["xfT_ps"], 1)

            def router_up(b):
                pe.wait_ge(S["xfT_sb"], b + 1)
                T.matmul(A3[:, :], wr1[:, :], xfT[:, :], start=True, stop=True).then_inc(S["r1_ps"], 1)

            def router_down(b):
                pe.wait_ge(S["r1_sb"], b + 1)
                for t in range(NT):
                    last = T.matmul(A0[:, t * E:(t + 1) * E], r1T[:, ts(t)], wr2[:, :], start=True, stop=True)
                last.then_inc(S["logit_ps"], 1)

            def turn_routing(b):
                pe.wait_ge(S["c_ready"], b + 1)
                for t in range(NT):
                    last = T.transpose(A1[0:E, ts(t)], c_sb[:, t, :], ident[:, :])
                last.then_inc(S["cT_ps"], 1)

            def weigh_biases(b):
                pe.wait_ge(S["cT_sb"], b + 1)
                T.matmul(A2[:, :], b2_sb[:, :], cT, start=True, stop=True).then_inc(S["init_ps"], 1)

            stages = {4: turn_xn, 6: quantum_query, 8: mean_key, 10: values, 12: coordinates, 14: spread,
                      16: distance(0), 18: scores(0), 19: distance(1), 21: scores(1), 22: distance(2), 24: scores(2),
                      25: distance(3), 27: scores(3), 31: transpose_prob, 35: weigh_values, 37: output,
                      45: turn_xf, 47: router_up, 49: router_down, 54: turn_routing, 56: weigh_biases}

            def last_turn(b):
                pe.wait_ge(S["y_done"], E * (b + 1))
                for t in range(NT):
                    last = T.transpose(A3[:, ts(t)], acc[:, ts(t)], ident[:, :])
                last.then_inc(S["fin_ps"], 1)

            final = {5: last_turn}

            def down(u, e, c):
                pe.wait_ge(S["split_ready"], FC * u + c + 1)
                if c == 0:
                    pe.wait_ge(S["y_free"], u + 1)
                y = YB[e % 2][:, :]
                T.matmul(y, w2_hi[:, e, c, :], h_hi[:, c, :], start=(c == 0), stop=False)
                T.matmul(y, w2_lo[:, e, c, :], h_hi[:, c, :], start=False, stop=False)
                T.matmul(y, w2_hi[:, e, c, :], h_lo[:, c, :], start=False, stop=(c == FC - 1)
                         ).then_inc(S["chunk_read"], 1)

            def ffn(b, k):
                e, c = divmod(k, FC)
                kk = SLOTS * b + k
                zero = isinstance(b, int) and b == 0
                if k == 0:
                    pe.wait_ge(S["xhi_ready"], b + 1)
                if zero and c == 0:
                    pe.wait_ge(S["w_lo_done"], e + 1)
                if not (zero and k < 2):
                    pe.wait_ge(S["g_ready"], kk - 1)
                T.matmul(HB[c % 2][:, :], w1_hi[:, e, ts(c)], x_hi[:, :], start=True, stop=False)
                T.matmul(HB[c % 2][:, :], w1_lo[:, e, ts(c)], x_hi[:, :], start=False, stop=False)
                if k == 0:
                    pe.wait_ge(S["xlo_ready"], b + 1)
                T.matmul(HB[c % 2][:, :], w1_hi[:, e, ts(c)], x_lo[:, :], start=False, stop=True).then_inc(S["h_ps"], 1)
                if e:
                    down(E * b + e - 1, e - 1, c)
                elif not zero:
                    down(E * b - 1, E - 1, c)

            iterations(pe, ffn, stages, final)
            for c in range(FC):
                down(E * B - 1, E - 1, c)
            last_turn(B - 1)


POOL_SETUP = 17
DVE_SETUP = 7
DVE_ORDER = 34
WEIGHTS_BEFORE_SOFTMAX = 16
PROLOGUE = {}
for _e in range(16):
    PROLOGUE.setdefault(1 + _e * 3 // 2, []).append(_e)

_INS = ["L0_attn_hidden_states", "L0_attn_Wq", "L0_attn_bq", "L0_attn_Wk", "L0_attn_bk", "L0_attn_Wv", "L0_attn_bv",
        "L0_attn_Wo", "L0_attn_bo", "L0_attn_Wtq", "L0_attn_btq", "L0_attn_Wfq", "L0_attn_bfq",
        "L0_ffn_Wr1", "L0_ffn_br1", "L0_ffn_Wr2", "L0_ffn_br2", "L0_ffn_W1", "L0_ffn_b1", "L0_ffn_W2", "L0_ffn_b2"]


def kernel(**inputs):
    import numpy as _np
    import concourse.bacc as _bacc
    from concourse import mybir as _mybir
    from concourse.bass_utils import run_bass_kernel_spmd as _run

    nc = _bacc.Bacc("TRN2", target_bir_lowering=False, num_devices=1)
    arrays, args = {}, []
    for name in _INS:
        a = _np.ascontiguousarray(inputs[name])
        arrays[f"in_{name}_dram"] = a
        args.append(nc.dram_tensor(f"in_{name}_dram", a.shape, _mybir.dt.from_np(a.dtype), kind="ExternalInput").ap())
    shape = inputs[_INS[0]].shape
    args.append(nc.dram_tensor("out_0_dram", tuple(shape), _mybir.dt.float32, kind="ExternalOutput").ap())
    attention_moe_kernel(nc, *args)
    r = _run(nc, [arrays], core_ids=[0])
    return r.results[0]["out_0_dram"]
```

```python
from contextlib import ExitStack

import concourse.bass as bass
from concourse import mybir

F32 = mybir.dt.float32
F32R = mybir.dt.float32r
BF16 = mybir.dt.bfloat16
U32 = mybir.dt.uint32
ALU = mybir.AluOpType
ACT = mybir.ActivationFunctionType
AX_X = mybir.AxisListType.X


P = 128
EPS = 1e-5
TINY_NORM = 1e-12
THRESHOLD_FACTOR = 1.25
QUANTUM = 0.1
PI_CONE = 2.0 ** -12
MASKED = -(2.0 ** 40)
EULER = 2.718281828459045
TOP = 4
CHUNK_LAG = 4
VECTOR_SLOTS = (10, 12, 30, 31, 32, 33, 34, 35, 36, 44, 51, 58, 59, 63)
SPARE_SLOTS = (32, 33)


NCOORD = 10
RAWS = 3
UPPER_SPLITS = {1: (0, 1), 3: (2,), 5: (3,), 9: (4,), 17: (5,), 20: (6,), 23: (7,), 34: (8, 9), 37: (10,), 38: (11,),
                44: (12, 13), 51: (14,), 52: (15,)}
LOWER_SPLITS = {0: (0, 1), 3: (2,), 5: (3,), 9: (4,), 27: (5, 6, 7, 8), 37: (9, 10), 42: (11,), 46: (12, 13),
                50: (14, 15)}
POOL_SETUP = 17
DVE_SETUP = 10
DVE_ORDER = 32


def attention_moe_kernel(nc, x_d, Wq, bq, Wk, bk, Wv, bv, Wo, bo, Wtq, btq, Wfq, bfq,
                         Wr1, br1, Wr2, br2, W1, b1, W2, b2, out_d):
    B, N, D = x_d.shape
    E, _, FF = W1.shape
    NT = N // P
    FC = FF // P
    SLOTS = E * FC
    assert D == P and N == 512 and FC == 4 and E == 16 and CHUNK_LAG == FC
    SCALE = float(D) ** -0.5
    PAIRS = float(N) * float(N)

    cT_d = nc.dram_tensor("routing_scratch", (E, B * N), F32, kind="Internal").ap()

    ctx = ExitStack()
    with ctx:
        def sb(name, shape, dt=F32):
            return ctx.enter_context(nc.sbuf_tensor(name, shape, dt))

        def sem(name):
            return ctx.enter_context(nc.semaphore(name))

        def ts(t):
            return slice(t * P, (t + 1) * P)

        def tiles(ap):
            return ap.rearrange("p (t d) -> p t d", t=NT)

        w1_hi = sb("w1_hi", [P, E, FF], F32R)
        w1_lo = sb("w1_lo", [P, E, FF], F32R)
        w2_hi = sb("w2_hi", [P, E, FC, P], F32R)
        w2_lo = sb("w2_lo", [P, E, FC, P], F32R)
        x_hi = sb("x_hi", [P, N], F32R)
        x_lo = sb("x_lo", [P, N], F32R)
        g = sb("g", [P, FC, N])
        h_hi = sb("h_hi", [P, FC, N], F32R)
        h_lo = sb("h_lo", [P, FC, N], F32R)
        acc = sb("acc", [P, N])
        c_bc = sb("c_bc", [P, 2, N])
        x_in = sb("x_in", [P, NT, P])
        x1 = sb("x1", [P, 2 * N])
        ident = sb("ident", [P, P])
        ones = sb("ones", [P, P])
        mask_w = sb("mask_w", [P, P], BF16)
        tri = sb("tri", [P, P], BF16)
        pick = sb("pick", [NCOORD, 2, P], F32R)
        iota_e = sb("iota_e", [P, E])
        half = sb("half", [P, NT])
        mhalf = sb("mhalf", [P, NT])
        euler = sb("euler", [P, NT * TOP])
        wT = sb("wT", [P, 4, P])
        wtqT = sb("wtqT", [P, 2])
        bk_scaled = sb("bk_scaled", [P, 1])
        cols = sb("cols", [P, 70])
        quant_cols = sb("quant_cols", [P, 3])
        wfq_raw = sb("wfq_raw", [P, 2])
        quant_w = sb("quant_w", [67, P])
        btq_bc = sb("btq_bc", [P, 2])
        br2_bc = sb("br2_bc", [P, E])
        wr1 = sb("wr1", [P, P])
        wr2 = sb("wr2", [P, E])
        b2_sb = sb("b2_sb", [E, P])
        st6 = sb("st6", [P, NT, 6])
        mv = sb("mv", [P, NT, 2])
        ve = sb("ve", [P, NT])
        rstd = sb("rstd", [P, NT])
        nmean = sb("nmean", [P, NT])
        fst6 = sb("fst6", [P, NT, 6])
        fmv = sb("fmv", [P, NT, 2])
        fve = sb("fve", [P, NT])
        frstd = sb("frstd", [P, NT])
        fnmean = sb("fnmean", [P, NT])
        xn = sb("xn", [P, NT, P])
        pick_raw = xn[0:NCOORD, 0:2, :]
        xnT = sb("xnT", [P, N])
        qT = sb("qT", [P, N])
        kT = sb("kT_xfT", [P, N])
        xfT = kT
        v_sb = sb("v_o", [P, NT, P])
        o_sb = v_sb[:, :, :]
        rows = v_sb
        xbc = sb("xbc_s", [P, N])
        s_sb = tiles(xbc[:, :])
        quer = s_sb[:, :, 0:NCOORD]
        dirs = s_sb[:, :, 32:35]
        keyc = s_sb[:, :, 64:64 + NCOORD]
        ybc = sb("ybc_r1T", [P, N])
        r1T = ybc
        cone = sb("cone", [P, N], BF16)
        mask = sb("mask", [P, N], BF16)
        prob = sb("prob_ady_cT", [P, N * 5 // 2])
        ady = prob[:, 0:N]
        cT = prob[0:E, 0:N]
        w_raw = prob[:, 0:N].rearrange("p (a d) -> p a d", a=4)
        wtq_row = prob[0:2, N:N + P]
        probT = sb("probT_hit", [P, N * 5 // 2])
        hit = probT[:, 0:NT * TOP * E].rearrange("p (k e) -> p k e", e=E)
        rT = probT[64:67, 0:N]
        turned = sb("turned", [NCOORD, 2, N], F32R)
        turned_queries = turned[:, 0, :]
        turned_keys = turned[:, 1, :]
        qp = sb("qp", [P, NT, 2])
        a = sb("a", [P, NT, 2])
        mean2 = sb("mean2", [P, 2])
        sq = sb("sq", [P, NT, 2])
        nrm = sb("nrm", [P, NT])
        rn = sb("rn", [P, NT])
        mom = sb("mom", [P, 4, NT])
        tot = sb("tot", [P, 4])
        sc = sb("sc", [P, 8])
        nay = sb("nay", [P, NT])
        ax12 = sb("ax12", [P, NT])
        lim = sb("lim", [P, NT])
        nmax = sb("nmax", [P, NT])
        rsum = sb("rsum", [P, NT])
        rinv = sb("rinv", [P, NT])
        lg = sb("lg", [P, NT, E])
        top8 = sb("top8", [P, NT, 8])
        idx8 = sb("idx8", [P, NT, 8], U32)
        idxf = sb("idxf", [P, NT, 8])
        dif = sb("dif", [P, NT * TOP])
        ew = sb("ew", [P, NT * TOP])
        esum = sb("esum", [P, NT])
        einv = sb("einv", [P, NT])
        c_sb = sb("c_sb", [P, NT, E])

        def bank(name):
            return ctx.enter_context(nc.psum_tensor(name, [P, 512], F32))

        A0, A1, A2, A3 = [bank(f"A{i}") for i in range(4)]
        HB = [bank(f"HB{i}") for i in range(2)]
        YB = [bank(f"YB{i}") for i in range(2)]

        SCORES = [A0[:, 0:P], A1[:, 0:2 * P], A0[:, P:4 * P], A2[:, 0:4 * P]]
        PB = [0, P, 3 * P, 6 * P]
        KB = [0, 4 * P, 7 * P, 9 * P]

        def keys(j, lo, hi):
            return probT[:, KB[j] + (lo - j) * P:KB[j] + (hi - j) * P]

        names = """consts_in consts_late pool_setup dve_setup pe_setup
            x_loaded x_stats ln_stats rstd_ready xn_ready xnT_ps xnT_sb
            qp_ps qp_sb q_ps q_sb k_ps k_sb v_ps v_ready mean_ps a_ready norm_ready rn_ready
            mom_ready mom_ps var_ready std_ready packed turned_ps turned_sb xbc_ps ybc_ps xybc_sb
            dist_ps ady_ready mask_ready score_ps nmax_ready exps_done quantum_ps probT_act probT_dve o_ps
            s_ready attention_normed x1_ready xf_ready xfT_ps xfT_sb xhi_ready xlo_ready
            r1_ps r1_sb logit_ps logit_sb dif_ready ew_ready c_ready cT_ps cT_sb cT_stored init_ps c_in0 c_in1
            w_in0 w_in1 w_in2 w_hi_done w_lo_done
            h_ps g_ready scalar_hi hi_ready split_ready chunk_read y_free y_done
            fin_ps fin_stats fin_rstd fin_normed fin_out stored
            pool_order dve_order fin_order dve_gate pool_gate sp_gate""".split()
        S = {n: sem(n) for n in names}

        block = ctx.enter_context(nc.Block())
        BIAS_COL = {"bq": 64, "bk": 65, "bv": 66, "bo": 67, "bfq": 68, "br1": 69}
        NROWS = 70
        NCONST = 4 + 1 + 1 + 6 + 1
        NLATE = 5

        def col(name):
            return cols[:, BIAS_COL[name]:BIAS_COL[name] + 1]

        def up_bank(k):
            return {SPARE_SLOTS[0]: A2, SPARE_SLOTS[1]: A1}.get(k, HB[k % 2])

        def scalar_slots(b, k):
            return (SLOTS - len(VECTOR_SLOTS)) * b + sum(i not in VECTOR_SLOTS for i in range(k + 1))

        def vector_slots(b, k):
            return len(VECTOR_SLOTS) * b + sum(i in VECTOR_SLOTS for i in range(k + 1))

        def x1_of(b):
            return tiles(x1[:, bass.ds((b % 2) * N, N)])

        def raw_of(e):
            return (c_bc[:, :, :], g[:, 0:2, :], g[:, 2:4, :])[e % RAWS].rearrange("p a n -> p (a n)")

        def run(ffn, att, fin, fb, stages, final, after=None, early=None, own=None):
            for k in range(SLOTS):
                if own and k in own:
                    own[k](fb)
                if ffn:
                    ffn(fb, k)
                if fin and k in final:
                    final[k](fb - 1)
                if att and k in stages:
                    stages[k](fb + 1)
                if early and k in early:
                    early[k](fb + 2)
                if after:
                    after(k)

        def iterations(eng, ffn, stages, final, prologue=None, early=None, own=None):
            run(None, True, False, -1, stages, final, prologue, early)
            run(ffn, True, False, 0, stages, final, None, early, own)
            last = B - 2 if early else B - 1
            with eng.Fori(1, last) as b:
                run(ffn, True, True, b, stages, final, None, early, own)
            for b in range(last, B):
                run(ffn, b < B - 1, True, b, stages, final, None, None, own)

        @block.sync
        def _(sp):
            n = 0

            def const(dst, src, name="consts_in"):
                nonlocal n
                sp.dma_start(dst, src).then_inc(S[name], 16)
                n += 1

            def load_x(b):
                src = x_d[b] if isinstance(b, int) else x_d[bass.ds(b, 1)].rearrange("o n d -> (o n) d")
                sp.dma_start(x_in[:, :, :], src.rearrange("(t p) d -> p t d", p=P)).then_inc(S["x_loaded"], 16)

            def load_w(e):
                raw = raw_of(e)
                if e >= RAWS:
                    sp.wait_ge(S["w_lo_done"], e - RAWS + 1)
                sp.dma_start(raw[:, 0:FF], W1[e]).then_inc(S[f"w_in{e % RAWS}"], 16)
                sp.dma_start(raw[:, FF:2 * FF].rearrange("p (c h) -> p c h", h=P),
                             W2[e].rearrange("(c p) h -> p c h", p=P)).then_inc(S[f"w_in{e % RAWS}"], 16)

            load_x(0)
            const(wtq_row, Wtq)
            const(rows[0:E * FC, 0, :], b1.rearrange("e (c p) -> (e c) p", p=P))
            for name, v in (("bq", bq), ("bk", bk), ("bv", bv), ("bo", bo), ("bfq", bfq), ("br1", br1)):
                const(rows[BIAS_COL[name]:BIAS_COL[name] + 1, 0, :], v.rearrange("(o d) -> o d", o=1))
            const(btq_bc[:, :], btq.partition_broadcast(P))
            assert n + 4 == NCONST
            load_w(0)
            for dst, src in ((wfq_raw[:, :], Wfq), (br2_bc[:, :], br2.partition_broadcast(P)), (wr1[:, :], Wr1),
                             (wr2[:, :], Wr2), (b2_sb[:, :], b2)):
                const(dst, src, "consts_late")
            assert n + 4 == NCONST + NLATE
            for e in range(1, E):
                load_w(e)

            def store_c(b):
                sp.wait_ge(S["cT_sb"], b + 1)
                sp.dma_start(cT_d[:, bass.ds(b * N, N)], cT).then_inc(S["cT_stored"], 16)

            def load_c(b, e):
                if not (isinstance(b, int) and b == 0 and e < 2):
                    sp.wait_ge(S["y_done"], E * b + e - 1)
                if e == 0:
                    sp.sem_inc(S["sp_gate"], 1)
                    sp.wait_ge(S["cT_stored"], 16 * b + 16)
                sp.dma_start(c_bc[:, e % 2, :], cT_d[e:e + 1, bass.ds(b * N, N)].broadcast_to([P, N])
                             ).then_inc(S[f"c_in{e % 2}"], 16)

            def iteration(b, att, fin):
                if not (isinstance(b, int) and b == 0):
                    store_c(b)
                    load_c(b, 0)
                    load_c(b, 1)
                for e in range(2, E):
                    load_c(b, e)
                    if e == 3 and fin:
                        sp.wait_ge(S["fin_out"], b)
                        sp.dma_start(out_d[bass.ds(b - 1, 1)].rearrange("o (t p) d -> p (o t) d", p=P), x1_of(b + 1)
                                     ).then_inc(S["stored"], 16)
                    if e == 10 and att == 2:
                        sp.wait_ge(S["x1_ready"], b + 2)
                        load_x(b + 2)

            sp.wait_ge(S["x1_ready"], 1)
            load_x(1)
            store_c(0)
            sp.wait_ge(S["w_lo_done"], E)
            load_c(0, 0)
            load_c(0, 1)
            iteration(0, 2, False)
            with sp.Fori(1, B - 2) as b:
                iteration(b, 2, True)
            iteration(B - 2, 1, True)
            iteration(B - 1, 0, True)
            sp.wait_ge(S["fin_out"], B)
            sp.dma_start(out_d[B - 1].rearrange("(t p) d -> p t d", p=P), x1_of(B - 1)).then_inc(S["stored"], 16)
            sp.wait_ge(S["stored"], 16 * B)

        @block.gpsimd
        def _(pool):
            G = nc.gpsimd
            order = 0

            def setup(ins):
                nonlocal order
                order += 1
                ins.then_inc(S["pool_setup"], 1)
                pool.wait_ge(S["pool_setup"], order)

            setup(G.memset(ident[:, :], 0.0))
            setup(G.affine_select(out=ident[:, :], in_=ident[:, :], compare_op=ALU.not_equal, fill=1.0, base=0,
                                  pattern=[[-1, P]], channel_multiplier=1))
            for tile, value in ((mask_w, 0.0), (tri, 0.0), (ones, 1.0), (half, 0.5), (mhalf, -0.5),
                                (euler, EULER), (xbc, 0.0)):
                setup(G.memset(tile[:, :], value))
            setup(G.memset(pick_raw, 0.0))
            for row in range(4):
                setup(G.affine_select(out=pick_raw[:, row % 2, :], in_=pick_raw[:, row % 2, :],
                                      compare_op=ALU.not_equal, fill=1.0, base=-row, pattern=[[0, P]],
                                      channel_multiplier=1))
            setup(G.affine_select(out=mask_w[:, :], in_=mask_w[:, :], compare_op=ALU.not_equal, fill=MASKED, base=0,
                                  pattern=[[-1, P]], channel_multiplier=1))
            setup(G.affine_select(out=tri[:, :], in_=tri[:, :], compare_op=ALU.is_ge, fill=1.0, base=0,
                                  pattern=[[-1, P]], channel_multiplier=1))
            setup(G.iota(iota_e[:, :], pattern=[[1, E]], base=0, channel_multiplier=0,
                         allow_small_or_imprecise_dtypes=True))
            assert order == POOL_SETUP

            def own_wait():
                pool.sem_inc(S["pool_gate"], 1)

            def inverse_std(src, tmp, dst, shift, order_value, dst_sem):
                own_wait()
                G.tensor_scalar(shift[:, :], src[:, :, 0], -1.0, None, ALU.mult)
                G.tensor_scalar(tmp[:, :], src[:, :, 1], EPS, None, ALU.add).then_inc(S["pool_order"], 1)
                pool.wait_ge(S["pool_order"], order_value - 1)
                G.tensor_tensor(dst[:, :], tmp[:, :], mhalf[:, :], ALU.pow).then_inc(S["pool_order"], 1)
                pool.wait_ge(S["pool_order"], order_value)
                G.tensor_tensor(shift[:, :], shift[:, :], dst[:, :], ALU.mult).then_inc(S[dst_sem], 1)

            def iteration(b, att, fin):
                done = 6 * b if att else 6 * B
                done_fin = 2 * (b - 2) if fin else 0
                if att:
                    pool.wait_ge(S["ln_stats"], 3 * b + 1)
                    inverse_std(mv, ve, rstd, nmean, done + done_fin + 2, "rstd_ready")
                    done = done + 2
                if not (isinstance(b, int) and b in (0, B + 1)):
                    pool.wait_ge(S["dif_ready"], b)
                    G.tensor_tensor(ew[:, :], euler[:, :], dif[:, :], ALU.pow).then_inc(S["ew_ready"], 1)
                if att:
                    pool.wait_ge(S["norm_ready"], b + 1)
                    G.tensor_tensor(rn[:, :], nrm[:, :], mhalf[:, :], ALU.pow).then_inc(S["rn_ready"], 1)
                if fin:
                    pool.wait_ge(S["fin_stats"], b - 1)
                    inverse_std(fmv, fve, frstd, fnmean, done + done_fin + 2, "fin_rstd")
                    done_fin = done_fin + 2
                if att:
                    pool.wait_ge(S["var_ready"], b + 1)
                    G.tensor_tensor(sc[:, 6:7], sc[:, 5:6], half[:, 0:1], ALU.pow).then_inc(S["std_ready"], 1)
                    for i in (2, 3):
                        pool.wait_ge(S["ln_stats"], 3 * b + i)
                        inverse_std(mv, ve, rstd, nmean, done + done_fin + 2 * i - 2, "rstd_ready")

            iteration(0, True, False)
            iteration(1, True, False)
            with pool.Fori(2, B) as b:
                iteration(b, True, True)
            iteration(B, False, True)
            iteration(B + 1, False, True)

        @block.vector
        def _(dve):
            V = nc.vector
            n = 0

            def setup(ins):
                nonlocal n
                n += 1
                ins.then_inc(S["dve_setup"], 1)

            def own_wait():
                dve.sem_inc(S["dve_gate"], 1)

            def stats(st, src):
                for t in range(NT):
                    last = V.bn_stats(st[:, t, :], src[:, t, :])
                return last

            def aggregate(m, st):
                own_wait()
                for t in range(NT):
                    last = V.bn_aggr(m[:, t, :], st[:, t, :])
                return last

            linked = {"n": 0}

            def link(b, ins):
                linked["n"] += 1
                ins.then_inc(S["dve_order"], 1)
                dve.wait_ge(S["dve_order"], b * DVE_ORDER + linked["n"])

            def norm_in(b):
                if not (isinstance(b, int) and b == 0):
                    dve.wait_ge(S["xf_ready"], b)
                    own_wait()
                dve.wait_ge(S["x_loaded"], 16 * b + 16)
                own_wait()
                stats(st6, x_in).then_inc(S["x_stats"], 1)
                dve.wait_ge(S["x_stats"], b + 1)
                aggregate(mv, st6).then_inc(S["ln_stats"], 1)

            def quantum(b):
                linked["n"] = 0
                dve.wait_ge(S["qp_ps"], b + 1)
                V.tensor_tensor(qp[:, :, :], A0[:, 0:2 * NT].rearrange("p (t c) -> p t c", c=2),
                                btq_bc[:, :].unsqueeze(1).broadcast_to([P, NT, 2]), ALU.add).then_inc(S["qp_sb"], 1)
                dve.wait_ge(S["qp_sb"], b + 1)
                link(b, V.tensor_tensor(sq[:, :, :], qp[:, :, :], qp[:, :, :], ALU.mult))
                link(b, V.tensor_tensor(nrm[:, :], sq[:, :, 0], sq[:, :, 1], ALU.add))
                V.tensor_scalar(nrm[:, :], nrm[:, :], TINY_NORM ** 2, None, ALU.max).then_inc(S["norm_ready"], 1)

            def centre(b):
                dve.wait_ge(S["mean_ps"], b + 1)
                link(b, V.tensor_reduce(mean2[:, :], A0[:, 2 * NT:4 * NT].rearrange("p (t c) -> p c t", c=2),
                                        AX_X, ALU.add))
                V.scalar_tensor_tensor(a[:, :, :], mean2[:, :].unsqueeze(1).broadcast_to([P, NT, 2]), -1.0 / N,
                                       qp[:, :, :], ALU.mult, ALU.add).then_inc(S["a_ready"], 1)

            def moments(b):
                dve.wait_ge(S["a_ready"], b + 1)
                V.tensor_tensor(mom[:, 0, :], a[:, :, 0], a[:, :, 0], ALU.mult)
                V.tensor_tensor(mom[:, 1, :], a[:, :, 1], a[:, :, 1], ALU.mult)
                V.tensor_copy(keyc[:, :, 0:2].bitcast(F32R), a[:, :, :])
                V.tensor_copy(keyc[:, :, 4:6].bitcast(F32R), a[:, :, :])
                V.tensor_copy(quer[:, :, 0:2].bitcast(F32R), a[:, :, :])
                V.tensor_copy(quer[:, :, 2:4].bitcast(F32R), a[:, :, :])
                V.tensor_copy(quer[:, :, 6:10], mhalf[:, :].unsqueeze(2).broadcast_to([P, NT, 4]))
                link(b, V.tensor_tensor(mom[:, 2, :], a[:, :, 0], a[:, :, 1], ALU.mult))
                V.tensor_tensor(keyc[:, :, 2:4].bitcast(F32R), a[:, :, :], keyc[:, :, 0:2], ALU.subtract)
                V.tensor_tensor(quer[:, :, 4:6].bitcast(F32R), a[:, :, :], keyc[:, :, 0:2], ALU.subtract)
                squares = mom[:, 0:2, :].rearrange("p c t -> p t c")
                V.tensor_copy(keyc[:, :, 6:8].bitcast(F32R), squares)
                dve.wait_ge(S["rn_ready"], b + 1)
                link(b, V.tensor_tensor(nrm[:, :], mom[:, 0, :], mom[:, 1, :], ALU.add))
                V.tensor_tensor(keyc[:, :, 8:10].bitcast(F32R), squares, keyc[:, :, 6:8], ALU.subtract)
                V.tensor_tensor(dirs[:, :, 0:2], qp[:, :, :], rn[:, :].unsqueeze(2).broadcast_to([P, NT, 2]),
                                ALU.mult)
                V.tensor_copy(dirs[:, :, 2:3], ones[:, 0:NT].unsqueeze(2)).then_inc(S["packed"], 1)
                V.tensor_tensor(mom[:, 3, :], nrm[:, :], nrm[:, :], ALU.mult).then_inc(S["mom_ready"], 1)
                V.tensor_scalar(nay[:, :], a[:, :, 1], -1.0, None, ALU.mult)
                V.tensor_scalar(ax12[:, :], a[:, :, 0], PI_CONE, None, ALU.mult)

            def variance(b):
                dve.wait_ge(S["mom_ps"], b + 1)
                link(b, V.tensor_reduce(tot[:, :], A0[:, 4 * NT:8 * NT].rearrange("p (q t) -> p q t", t=NT),
                                        AX_X, ALU.add))
                sxx, syy, sxy, snn = (tot[:, i:i + 1] for i in range(4))
                link(b, V.tensor_tensor(sc[:, 0:1], sxx, syy, ALU.add))
                link(b, V.scalar_tensor_tensor(sc[:, 1:2], sc[:, 0:1], -0.5, sc[:, 0:1], ALU.mult, ALU.mult))
                link(b, V.scalar_tensor_tensor(sc[:, 1:2], snn, N / 2.0, sc[:, 1:2], ALU.mult, ALU.add))
                link(b, V.scalar_tensor_tensor(sc[:, 2:3], sxx, sxx, sc[:, 1:2], ALU.mult, ALU.add))
                link(b, V.scalar_tensor_tensor(sc[:, 3:4], syy, syy, sc[:, 2:3], ALU.mult, ALU.add))
                link(b, V.tensor_tensor(sc[:, 4:5], sxy, sxy, ALU.mult))
                link(b, V.scalar_tensor_tensor(sc[:, 4:5], sc[:, 4:5], 2.0, sc[:, 3:4], ALU.mult, ALU.add))
                V.tensor_scalar(sc[:, 5:6], sc[:, 4:5], 4.0 / (PAIRS - 1.0), 0.0, ALU.mult, ALU.max
                                ).then_inc(S["var_ready"], 1)

            def threshold(b):
                dve.wait_ge(S["std_ready"], b + 1)
                link(b, V.tensor_scalar(sc[:, 7:8], sc[:, 6:7], THRESHOLD_FACTOR, None, ALU.mult))
                link(b, V.scalar_tensor_tensor(sc[:, 7:8], sc[:, 0:1], 2.0 / N, sc[:, 7:8], ALU.mult, ALU.add))
                link(b, V.tensor_scalar(lim[:, :], nrm[:, :], sc[:, 7:8], 0.5, ALU.subtract, ALU.mult))

            def pair_mask(t):
                def stage(b):
                    w = P * (t + 1)
                    dve.wait_ge(S["ady_ready"], NT * b + t + 1)
                    link(b, V.scalar_tensor_tensor(cone[:, 0:w], xbc[:, 0:w], ax12[:, t:t + 1], ady[:, 0:w],
                                                   ALU.subtract, ALU.is_gt))
                    if t >= 1:
                        dve.wait_ge(S["score_ps"], NT * b + t)
                    dve.wait_ge(S["dist_ps"], NT * b + t + 1)
                    V.scalar_tensor_tensor(mask[:, 0:w], A3[:, 0:w], lim[:, t:t + 1], cone[:, 0:w],
                                           ALU.is_lt, ALU.max).then_inc(S["mask_ready"], 1)
                return stage

            def row_max(t):
                def stage(b):
                    dve.wait_ge(S["score_ps"], NT * b + t + 1)
                    V.tensor_reduce(nmax[:, t:t + 1], SCORES[t], AX_X, ALU.max, negate=True).then_inc(S["nmax_ready"], 1)
                return stage

            def turn_prob(b):
                dve.wait_ge(S["quantum_ps"], b + 1)
                for j in range(3):
                    last = V.tensor_copy(keys(j, 2, 3), A1[:, ts(j)])
                last.then_inc(S["probT_dve"], 1)

            def residual(b):
                dve.wait_ge(S["exps_done"], 4 * b + 4)
                link(b, V.reciprocal(rinv[:, :], rsum[:, :]))
                dve.wait_ge(S["o_ps"], b + 1)
                for t in range(NT):
                    last = V.scalar_tensor_tensor(s_sb[:, t, :], A1[:, ts(t)], rinv[:, t:t + 1], xn[:, t, :],
                                                  ALU.mult, ALU.add)
                link(b, last)
                V.tensor_tensor(s_sb, tiles(A3[:, :]), s_sb, ALU.add).then_inc(S["s_ready"], 1)

            def norm_attention(b):
                dve.wait_ge(S["s_ready"], b + 1)
                own_wait()
                link(b, stats(st6, s_sb))
                aggregate(mv, st6).then_inc(S["ln_stats"], 1)

            def add_attention(b):
                dve.wait_ge(S["attention_normed"], b + 1)
                if not (isinstance(b, int) and b < 2):
                    dve.wait_ge(S["stored"], 16 * (b - 1))
                V.tensor_tensor(x1_of(b), x_in[:, :, :], s_sb, ALU.add).then_inc(S["x1_ready"], 1)

            def norm_ffn(b):
                dve.wait_ge(S["x1_ready"], b + 1)
                own_wait()
                link(b, stats(st6, x1_of(b)))
                aggregate(mv, st6).then_inc(S["ln_stats"], 1)

            def choose(b):
                dve.wait_ge(S["logit_ps"], b + 1)
                V.tensor_tensor(lg[:, :, :], A0[:, 0:NT * E].rearrange("p (t e) -> p t e", e=E),
                                br2_bc[:, :].unsqueeze(1).broadcast_to([P, NT, E]), ALU.add).then_inc(S["logit_sb"], 1)
                dve.wait_ge(S["logit_sb"], b + 1)
                own_wait()
                for t in range(NT):
                    last = V.max(top8[:, t, :], lg[:, t, :])
                link(b, last)
                V.tensor_tensor(dif[:, :].rearrange("p (t k) -> p t k", k=TOP), top8[:, :, 0:TOP],
                                top8[:, :, 0:1].broadcast_to([P, NT, TOP]), ALU.subtract).then_inc(S["dif_ready"], 1)

            def chosen(b):
                for t in range(NT):
                    last = V.max_index(idx8[:, t, :], top8[:, t, :], lg[:, t, :])
                link(b, last)
                link(b, V.tensor_copy(idxf[:, :, :], idx8[:, :, :]))
                h4 = hit.rearrange("p (t k) e -> p t k e", k=TOP)
                for t in range(NT):
                    last = V.tensor_tensor(h4[:, t], idxf[:, t, 0:TOP].unsqueeze(2).broadcast_to([P, TOP, E]),
                                           iota_e[:, :].unsqueeze(1).broadcast_to([P, TOP, E]), ALU.is_equal)
                link(b, last)

            def routing(b):
                dve.wait_ge(S["ew_ready"], b + 1)
                ew4 = ew[:, :].rearrange("p (t k) -> p t k", k=TOP)
                link(b, V.tensor_reduce(esum[:, :], ew4, AX_X, ALU.add))
                link(b, V.reciprocal(einv[:, :], esum[:, :]))
                link(b, V.tensor_tensor(ew4, ew4, einv[:, :].unsqueeze(2).broadcast_to([P, NT, TOP]), ALU.mult))
                link(b, V.tensor_tensor(hit, hit, ew[:, :].unsqueeze(2).broadcast_to([P, NT * TOP, E]), ALU.mult))
                V.tensor_reduce(c_sb[:, :, :], hit.rearrange("p (t k) e -> p t e k", k=TOP), AX_X, ALU.add
                                ).then_inc(S["c_ready"], 1)
                assert linked["n"] == DVE_ORDER, linked

            def turn_routing(b):
                dve.wait_ge(S["cT_ps"], b + 1)
                V.tensor_copy(cT, A1[0:E, :]).then_inc(S["cT_sb"], 1)

            def split_input(b):
                dve.wait_ge(S["xhi_ready"], b + 1)
                V.tensor_tensor(x_lo[:, :], xfT[:, :], x_hi[:, :].bitcast(F32), ALU.subtract
                                ).then_inc(S["xlo_ready"], 1)

            stages = {3: quantum, 5: centre, 6: moments, 9: variance, 12: threshold,
                      14: pair_mask(0), 17: pair_mask(1), 18: row_max(0), 20: pair_mask(2), 21: row_max(1),
                      23: pair_mask(3), 24: row_max(2), 27: row_max(3), 37: turn_prob, 39: residual,
                      40: norm_attention, 45: add_attention, 46: norm_ffn, 58: choose,
                      62: split_input}
            early = {54: norm_in}
            own = {0: chosen, 1: routing, 4: turn_routing}

            def last_stats(b):
                dve.wait_ge(S["fin_ps"], b + 1)
                own_wait()
                stats(fst6, tiles(A3[:, :])).then_inc(S["fin_order"], 1)
                dve.wait_ge(S["fin_order"], b + 1)
                aggregate(fmv, fst6).then_inc(S["fin_stats"], 1)

            def last_norm(b):
                dve.wait_ge(S["fin_normed"], b + 1)
                V.tensor_tensor(x1_of(b), o_sb, x1_of(b), ALU.add).then_inc(S["fin_out"], 1)

            final = {7: last_stats, 13: last_norm}

            def accumulate(u, b, e):
                dve.wait_ge(S["chunk_read"], FC * (u + 1))
                dve.wait_ge(S[f"c_in{e % 2}"], 8 * E * b + 16 * (e // 2 + 1))
                yc = c_bc[:, e % 2, :]
                V.tensor_tensor(yc, YB[e % 2][:, :], yc, ALU.mult).then_inc(S["y_free"], 1)
                dve.wait_ge(S["y_free"], 2 + u + 1)
                if e == 0:
                    dve.wait_ge(S["init_ps"], b + 1)
                V.tensor_tensor(acc[:, :], (acc if e else A2)[:, :], yc, ALU.add).then_inc(S["y_done"], 1)

            def ffn(b, k):
                e, c = divmod(k, FC)
                kk = SLOTS * b + k
                first = isinstance(b, int) and kk < FC
                if k in VECTOR_SLOTS:
                    dve.wait_ge(S["g_ready"], kk + 1)
                    V.tensor_copy(h_hi[:, c, :], g[:, c, :]).then_inc(S["hi_ready"], 1)
                    dve.wait_ge(S["hi_ready"], vector_slots(b, k))
                else:
                    dve.wait_ge(S["scalar_hi"], scalar_slots(b, k))
                V.tensor_tensor(h_lo[:, c, :], g[:, c, :], h_hi[:, c, :].bitcast(F32), ALU.subtract
                                ).then_inc(S["split_ready"], 1)
                if c == FC - 1 and not first:
                    if e:
                        accumulate(E * b + e - 1, b, e - 1)
                    elif not (isinstance(b, int) and b == 0):
                        accumulate(E * b - 1, b - 1, E - 1)

            def prologue(k):
                if k == 6:
                    setup_output_bias()
                if k == 10:
                    setup_quantum()
                for e in LOWER_SPLITS.get(k, ()):
                    raw = raw_of(e)
                    dve.wait_ge(S["w_hi_done"], e + 1)
                    V.tensor_tensor(w1_lo[:, e, :], raw[:, 0:FF], w1_hi[:, e, :].bitcast(F32), ALU.subtract)
                    V.tensor_tensor(w2_lo[:, e, :, :].rearrange("p c h -> p (c h)"), raw[:, FF:2 * FF],
                                    w2_hi[:, e, :, :].rearrange("p c h -> p (c h)").bitcast(F32), ALU.subtract
                                    ).then_inc(S["w_lo_done"], 1)

            def setup_output_bias():
                dve.wait_ge(S["consts_late"], 16 * NLATE)
                setup(V.tensor_scalar(quant_cols[:, 0:2], wfq_raw[:, :], QUANTUM, None, ALU.mult))
                dve.wait_ge(S["pe_setup"], 2)
                setup(V.tensor_tensor(quant_cols[:, 2:3], A2[:, 0:1], col("bo"), ALU.add))
                setup(V.tensor_copy(wT[:, 2, :], A3[:, 0:P]))
                dve.wait_ge(S["dve_setup"], 8)
                setup(V.scalar_tensor_tensor(quant_cols[:, 2:3], col("bfq"), QUANTUM, quant_cols[:, 2:3],
                                             ALU.mult, ALU.add))

            def setup_quantum():
                dve.wait_ge(S["pe_setup"], 3)
                setup(V.tensor_copy(quant_w[64:67, :], A3[0:3, P:2 * P]))
                assert n == DVE_SETUP

            dve.wait_ge(S["pool_setup"], POOL_SETUP)
            setup(V.tensor_copy(pick[:, :, :], pick_raw))
            norm_in(0)
            dve.wait_ge(S["pe_setup"], 1)
            setup(V.tensor_copy(wT[:, :, :].rearrange("p a d -> p (a d)"), A0[:, :]))
            setup(V.tensor_copy(wtqT[:, :], A1[:, 0:2]))
            setup(V.tensor_copy(cols[:, 0:NROWS], A1[:, P:P + NROWS]))
            dve.wait_ge(S["dve_setup"], 4)
            setup(V.tensor_scalar(bk_scaled[:, :], col("bk"), SCALE, None, ALU.mult))
            dve.sem_inc(S["y_free"], 2)
            iterations(dve, ffn, stages, final, prologue, early, own)
            dve.wait_ge(S["y_done"], E * B - 1)
            accumulate(E * B - 1, B - 1, E - 1)
            last_stats(B - 1)
            last_norm(B - 1)

        @block.scalar
        def _(act):
            A = nc.scalar
            for i, w in enumerate((Wq, Wk, Wv, Wo)):
                act.dma_start(w_raw[:, i, :], w).then_inc(S["consts_in"], 16)

            def normalise(dst, src, scale, shift):
                for t in range(NT):
                    last = A.activation(dst[:, t, :], src[:, t, :], ACT.Identity, bias=shift[:, t:t + 1],
                                        scale=scale[:, t:t + 1])
                return last

            def norm_input(b):
                act.wait_ge(S["rstd_ready"], 3 * b + 1)
                normalise(xn, x_in, rstd, nmean).then_inc(S["xn_ready"], 1)

            def normed_attention(b):
                act.wait_ge(S["rstd_ready"], 3 * b + 2)
                normalise(s_sb, s_sb, rstd, nmean).then_inc(S["attention_normed"], 1)

            def ffn_input(b):
                act.wait_ge(S["rstd_ready"], 3 * b + 3)
                normalise(s_sb, x1_of(b), rstd, nmean).then_inc(S["xf_ready"], 1)

            def last_normed(b):
                act.wait_ge(S["fin_rstd"], b + 1)
                normalise(o_sb, tiles(A3[:, :]), frstd, fnmean).then_inc(S["fin_normed"], 1)

            def key(b):
                act.wait_ge(S["k_ps"], b + 1)
                A.activation(kT[:, :], A2[:, :], ACT.Identity, bias=bk_scaled[:, :], scale=SCALE
                             ).then_inc(S["k_sb"], 1)

            def upper_input(b):
                if not (isinstance(b, int) and b == 0):
                    act.wait_ge(S["h_ps"], SLOTS * b)
                A.copy(x_hi[:, :], xfT[:, :]).then_inc(S["xhi_ready"], 1)

            def turned_xn(b):
                act.wait_ge(S["xnT_ps"], b + 1)
                A.copy(xnT[:, :], A0[:, :]).then_inc(S["xnT_sb"], 1)

            def query(b):
                act.wait_ge(S["q_ps"], b + 1)
                A.activation(qT[:, :], A1[:, :], ACT.Identity, bias=col("bq")).then_inc(S["q_sb"], 1)

            def value(b):
                act.wait_ge(S["v_ps"], b + 1)
                if not (isinstance(b, int) and b < 2):
                    act.wait_ge(S["fin_out"], b - 1)
                A.copy(v_sb[:, :, :].rearrange("p t d -> p (t d)"), A3[:, :]).then_inc(S["v_ready"], 1)

            def coordinate_rows(b):
                act.wait_ge(S["turned_ps"], b + 1)
                A.copy(turned_keys, A1[64:64 + NCOORD, :])
                A.copy(turned_queries, A1[0:NCOORD, :])
                A.copy(rT, A1[32:35, :]).then_inc(S["turned_sb"], 1)

            def coordinate_tiles(b):
                act.wait_ge(S["xbc_ps"], b + 1)
                A.mul(xbc[:, :], A1[:, :], PI_CONE)
                act.wait_ge(S["ybc_ps"], b + 1)
                A.copy(ybc[:, :], A2[:, :]).then_inc(S["xybc_sb"], 1)

            def abs_dy(t):
                def stage(b):
                    w = P * (t + 1)
                    if t == 0:
                        act.wait_ge(S["xybc_sb"], b + 1)
                        act.wait_ge(S["var_ready"], b + 1)
                        if not (isinstance(b, int) and b == 0):
                            act.wait_ge(S["cT_stored"], 16 * b)
                    else:
                        act.wait_ge(S["mask_ready"], NT * b + t)
                    A.activation(ady[:, 0:w], ybc[:, 0:w], ACT.Abs, bias=nay[:, t:t + 1]).then_inc(S["ady_ready"], 1)
                return stage

            def softmax(b):
                act.wait_ge(S["nmax_ready"], NT * b + NT)
                for t in (3, 1, 2, 0):
                    m = A.activation(prob[:, PB[t]:PB[t] + P * (t + 1)], SCORES[t], ACT.Exp, bias=nmax[:, t:t + 1],
                                     accum_out=rsum[:, t:t + 1]).then_inc(S["exps_done"], 1)

            def turn_prob3(b):
                act.wait_ge(S["quantum_ps"], b + 1)
                for j in range(NT):
                    m = A.copy(keys(j, 3, 4), A0[:, ts(j)])
                m.then_inc(S["probT_act"], 1)

            def turn_prob01(b):
                A.copy(keys(0, 0, 2), A2[:, 0:2 * P])
                A.copy(keys(1, 1, 2), A2[:, 2 * P:3 * P]).then_inc(S["probT_act"], 1)

            def turned_xf(b):
                act.wait_ge(S["xfT_ps"], b + 1)
                A.copy(xfT[:, :], A2[:, :]).then_inc(S["xfT_sb"], 1)

            def router_hidden(b):
                act.wait_ge(S["r1_ps"], b + 1)
                A.activation(r1T[:, :], A3[:, :], ACT.Relu, bias=col("br1")).then_inc(S["r1_sb"], 1)

            stages = {1: turned_xn, 7: query, 9: coordinate_rows, 11: coordinate_tiles, 13: key,
                      14: abs_dy(0), 17: abs_dy(1), 20: abs_dy(2), 23: abs_dy(3),
                      29: softmax, 34: value, 36: turn_prob3, 37: turn_prob01, 44: normed_attention, 51: ffn_input,
                      53: turned_xf, 55: router_hidden, 62: upper_input}
            early = {58: norm_input}
            final = {12: last_normed}

            def ffn(b, k):
                e, c = divmod(k, FC)
                kk = SLOTS * b + k
                act.wait_ge(S["h_ps"], kk + 1)
                A.activation(g[:, c, :], up_bank(k)[:, :], ACT.Gelu, bias=cols[:, k:k + 1]).then_inc(S["g_ready"], 1)
                if k not in VECTOR_SLOTS:
                    act.wait_ge(S["g_ready"], kk + 1)
                    A.copy(h_hi[:, c, :], g[:, c, :]).then_inc(S["scalar_hi"], 1)

            def prologue(k):
                for e in UPPER_SPLITS.get(k, ()):
                    raw = raw_of(e)
                    act.wait_ge(S[f"w_in{e % RAWS}"], 32 * (e // RAWS + 1))
                    A.copy(w1_hi[:, e, :], raw[:, 0:FF])
                    A.copy(w2_hi[:, e, :, :].rearrange("p c h -> p (c h)"), raw[:, FF:2 * FF]
                           ).then_inc(S["w_hi_done"], 1)

            act.wait_ge(S["dve_setup"], 1)
            norm_input(0)
            act.wait_ge(S["dve_setup"], 5)
            iterations(act, ffn, stages, final, prologue, early)
            last_normed(B - 1)

        @block.tensor
        def _(pe):
            T = nc.tensor
            pe.wait_ge(S["consts_in"], 16 * NCONST)
            pe.wait_ge(S["pool_setup"], POOL_SETUP)
            for i in range(4):
                T.transpose(A0[:, ts(i)], w_raw[:, i, :], ident[:, :])
            T.transpose(A1[:, 0:2], wtq_row, ident[0:2, 0:2])
            T.transpose(A1[:, P:P + NROWS], rows[0:NROWS, 0, :], ident[0:NROWS, 0:NROWS]).then_inc(S["pe_setup"], 1)
            pe.wait_ge(S["dve_setup"], 4)
            T.matmul(A3[:, 0:P], w_raw[:, 2, :], wT[:, 3, :], start=True, stop=True)
            T.matmul(A2[:, 0:1], wT[:, 3, :], col("bv"), start=True, stop=True).then_inc(S["pe_setup"], 1)

            def prologue(k):
                if k == 9:
                    pe.wait_ge(S["dve_setup"], 9)
                    T.transpose(A3[0:3, P:2 * P], quant_cols[:, :], ident[:, :]).then_inc(S["pe_setup"], 1)
                if k == 13:
                    pe.wait_ge(S["dve_setup"], DVE_SETUP)

            def turn_xn(b):
                pe.wait_ge(S["xn_ready"], b + 1)
                if not (isinstance(b, int) and b == 0):
                    pe.wait_ge(S["logit_sb"], b)
                for t in range(NT):
                    last = T.transpose(A0[:, ts(t)], xn[:, t, :], ident[:, :])
                last.then_inc(S["xnT_ps"], 1)

            def quantum_query(b):
                pe.wait_ge(S["xnT_sb"], b + 1)
                for t in range(NT):
                    last = T.matmul(A0[:, 2 * t:2 * t + 2], xnT[:, ts(t)], wtqT[:, :], start=True, stop=True)
                last.then_inc(S["qp_ps"], 1)

            def query(b):
                if not (isinstance(b, int) and b == 0):
                    pe.wait_ge(S["cT_sb"], b)
                T.matmul(A1[:, :], wT[:, 0, :], xnT[:, :], start=True, stop=True).then_inc(S["q_ps"], 1)

            def mean(b):
                pe.wait_ge(S["qp_sb"], b + 1)
                T.matmul(A0[:, 2 * NT:4 * NT], ones[:, :], qp[:, :, :].rearrange("p t c -> p (t c)"),
                         start=True, stop=True).then_inc(S["mean_ps"], 1)

            def key(b):
                pe.wait_ge(S["xybc_sb"], b + 1)
                T.matmul(A2[:, :], wT[:, 1, :], xnT[:, :], start=True, stop=True).then_inc(S["k_ps"], 1)

            def values(b):
                for t in range(NT):
                    last = T.matmul(A3[:, ts(t)], xnT[:, ts(t)], wT[:, 2, :], start=True, stop=True)
                last.then_inc(S["v_ps"], 1)

            def coordinates(b):
                pe.wait_ge(S["packed"], b + 1)
                pe.wait_ge(S["q_sb"], b + 1)
                for t in range(NT):
                    last = T.transpose(A1[0:64 + NCOORD, ts(t)], s_sb[:, t, 0:64 + NCOORD], ident[:, :])
                last.then_inc(S["turned_ps"], 1)
                pe.wait_ge(S["mom_ready"], b + 1)
                T.matmul(A0[:, 4 * NT:8 * NT], ones[:, :], mom[:, :, :].rearrange("p q t -> p (q t)"),
                         start=True, stop=True).then_inc(S["mom_ps"], 1)

            def spread(b):
                pe.wait_ge(S["turned_sb"], b + 1)
                T.matmul(A1[:, :], pick[:, 0, :], turned_keys, start=True, stop=True).then_inc(S["xbc_ps"], 1)
                if not (isinstance(b, int) and b == 0):
                    pe.wait_ge(S["y_done"], E * (b - 1) + 1)
                T.matmul(A2[:, :], pick[:, 1, :], turned_keys, start=True, stop=True).then_inc(S["ybc_ps"], 1)

            def distance(t):
                def stage(b):
                    w = P * (t + 1)
                    if t > 0:
                        pe.wait_ge(S["mask_ready"], NT * b + t)
                    elif not (isinstance(b, int) and b < 2):
                        pe.wait_ge(S["fin_normed"], b - 1)
                    T.matmul(A3[:, 0:w], turned_queries[:, ts(t)], turned_keys[:, 0:w], start=True, stop=True
                             ).then_inc(S["dist_ps"], 1)
                return stage

            def scores(t):
                def stage(b):
                    w = P * (t + 1)
                    s = SCORES[t]
                    if t == 0:
                        pe.wait_ge(S["var_ready"], b + 1)
                        pe.wait_ge(S["xybc_sb"], b + 1)
                    if t == 2:
                        pe.wait_ge(S["nmax_ready"], NT * b + 1)
                    T.matmul(s, qT[:, ts(t)], kT[:, 0:w], start=True, stop=False)
                    T.matmul(s[:, ts(t)], mask_w[:, :], tri[:, :], start=False, stop=False)
                    pe.wait_ge(S["mask_ready"], NT * b + t + 1)
                    T.matmul(s, mask_w[:, :], mask[:, 0:w], start=False, stop=True).then_inc(S["score_ps"], 1)
                return stage

            def scores_then_distance(t):
                def stage(b):
                    distance(t + 1)(b)
                    scores(t)(b)
                return stage

            def transpose_prob(b):
                pe.wait_ge(S["exps_done"], 4 * b + 4)
                for t, dst in ((3, [A0[:, ts(j)] for j in range(4)]), (2, [A1[:, ts(j)] for j in range(3)])):
                    if t == 2 and not (isinstance(b, int) and b == 0):
                        pe.wait_ge(S["g_ready"], SLOTS * (b - 1) + SPARE_SLOTS[1] + 1)
                    for j in range(t + 1):
                        T.transpose(dst[j], prob[:, PB[t] + j * P:PB[t] + (j + 1) * P], ident[:, :])
                if not (isinstance(b, int) and b == 0):
                    pe.wait_ge(S["g_ready"], SLOTS * (b - 1) + SPARE_SLOTS[0] + 1)
                T.transpose(A2[:, ts(0)], prob[:, PB[0]:PB[0] + P], ident[:, :])
                T.transpose(A2[:, ts(1)], prob[:, PB[1]:PB[1] + P], ident[:, :])
                T.transpose(A2[:, ts(2)], prob[:, PB[1] + P:PB[1] + 2 * P], ident[:, :])

            def quantum_output(b):
                pe.wait_ge(S["v_ready"], b + 1)
                for t in range(NT):
                    last = T.matmul(A3[:, ts(t)], rT[:, ts(t)], quant_w[64:67, :], start=True, stop=True)
                last.then_inc(S["quantum_ps"], 1)

            def weigh_values(b):
                pe.wait_ge(S["probT_act"], 2 * b + 2)
                pe.wait_ge(S["probT_dve"], b + 1)
                for t in range(NT):
                    for j in range(t + 1):
                        last = T.matmul(A1[:, ts(t)], keys(j, t, t + 1), v_sb[:, j, :], start=(j == 0), stop=(j == t))
                last.then_inc(S["o_ps"], 1)

            def turn_xf(b):
                pe.wait_ge(S["xf_ready"], b + 1)
                for t in range(NT):
                    last = T.transpose(A2[:, ts(t)], s_sb[:, t, :], ident[:, :])
                last.then_inc(S["xfT_ps"], 1)

            def router_up(b):
                pe.wait_ge(S["xfT_sb"], b + 1)
                T.matmul(A3[:, :], wr1[:, :], xfT[:, :], start=True, stop=True).then_inc(S["r1_ps"], 1)

            def router_down(b):
                pe.wait_ge(S["r1_sb"], b + 1)
                for t in range(NT):
                    last = T.matmul(A0[:, t * E:(t + 1) * E], r1T[:, ts(t)], wr2[:, :], start=True, stop=True)
                last.then_inc(S["logit_ps"], 1)

            def turn_routing(b):
                pe.wait_ge(S["c_ready"], b + 1)
                for t in range(NT):
                    last = T.transpose(A1[0:E, ts(t)], c_sb[:, t, :], ident[:, :])
                last.then_inc(S["cT_ps"], 1)

            def weigh_biases(b):
                pe.wait_ge(S["cT_sb"], b + 1)
                T.matmul(A2[:, :], b2_sb[:, :], cT, start=True, stop=True).then_inc(S["init_ps"], 1)

            stages = {1: turn_xn, 3: quantum_query, 5: mean, 7: query, 9: coordinates, 11: spread, 13: key,
                      14: distance(0), 17: scores_then_distance(0), 20: scores_then_distance(1),
                      23: scores_then_distance(2), 26: scores(3), 32: values, 35: transpose_prob, 36: quantum_output,
                      39: weigh_values, 53: turn_xf, 55: router_up, 57: router_down}
            own = {4: turn_routing, 7: weigh_biases}

            def last_turn(b):
                pe.wait_ge(S["y_done"], E * (b + 1))
                for t in range(NT):
                    last = T.transpose(A3[:, ts(t)], acc[:, ts(t)], ident[:, :])
                last.then_inc(S["fin_ps"], 1)

            final = {6: last_turn}

            def down(u, e, c):
                pe.wait_ge(S["split_ready"], FC * u + c + 1)
                if c == 0:
                    pe.wait_ge(S["y_free"], u + 1)
                y = YB[e % 2][:, :]
                T.matmul(y, w2_hi[:, e, c, :], h_hi[:, c, :], start=(c == 0), stop=False)
                T.matmul(y, w2_lo[:, e, c, :], h_hi[:, c, :], start=False, stop=False)
                T.matmul(y, w2_hi[:, e, c, :], h_lo[:, c, :], start=False, stop=(c == FC - 1)
                         ).then_inc(S["chunk_read"], 1)

            def ffn(b, k):
                e, c = divmod(k, FC)
                kk = SLOTS * b + k
                zero = isinstance(b, int) and b == 0
                if e:
                    down(E * b + e - 1, e - 1, c)
                elif not zero:
                    down(E * b - 1, E - 1, c)
                if k == 0:
                    pe.wait_ge(S["xhi_ready"], b + 1)
                if zero and c == 0:
                    pe.wait_ge(S["w_lo_done"], e + 1)
                h = up_bank(k)[:, :]
                if k in SPARE_SLOTS:
                    if not (isinstance(b, int) and b == B - 1):
                        pe.wait_ge(S["exps_done"], 4 * (b + 1) + 1 + SPARE_SLOTS.index(k))
                elif not (zero and k < 2):
                    pe.wait_ge(S["g_ready"], kk - (3 if k - 2 in SPARE_SLOTS else 1))
                T.matmul(h, w1_hi[:, e, ts(c)], x_hi[:, :], start=True, stop=False)
                T.matmul(h, w1_lo[:, e, ts(c)], x_hi[:, :], start=False, stop=False)
                if k == 0:
                    pe.wait_ge(S["xlo_ready"], b + 1)
                T.matmul(h, w1_hi[:, e, ts(c)], x_lo[:, :], start=False, stop=True).then_inc(S["h_ps"], 1)

            iterations(pe, ffn, stages, final, prologue, own=own)
            for c in range(FC):
                down(E * B - 1, E - 1, c)
            last_turn(B - 1)

_INS = ["L0_attn_hidden_states", "L0_attn_Wq", "L0_attn_bq", "L0_attn_Wk", "L0_attn_bk", "L0_attn_Wv", "L0_attn_bv",
        "L0_attn_Wo", "L0_attn_bo", "L0_attn_Wtq", "L0_attn_btq", "L0_attn_Wfq", "L0_attn_bfq",
        "L0_ffn_Wr1", "L0_ffn_br1", "L0_ffn_Wr2", "L0_ffn_br2", "L0_ffn_W1", "L0_ffn_b1", "L0_ffn_W2", "L0_ffn_b2"]


def kernel(**inputs):
    import numpy as _np
    import concourse.bacc as _bacc
    from concourse import mybir as _mybir
    from concourse.bass_utils import run_bass_kernel_spmd as _run

    nc = _bacc.Bacc("TRN2", target_bir_lowering=False, num_devices=1)
    arrays, args = {}, []
    for name in _INS:
        a = _np.ascontiguousarray(inputs[name])
        arrays[f"in_{name}_dram"] = a
        args.append(nc.dram_tensor(f"in_{name}_dram", a.shape, _mybir.dt.from_np(a.dtype), kind="ExternalInput").ap())
    shape = inputs[_INS[0]].shape
    args.append(nc.dram_tensor("out_0_dram", tuple(shape), _mybir.dt.float32, kind="ExternalOutput").ap())
    attention_moe_kernel(nc, *args)
    r = _run(nc, [arrays], core_ids=[0])
    return r.results[0]["out_0_dram"]
```
